# Optimizing a Trainium2 kernel written in Bass

```python
import numpy as np
import jax
import jax.numpy as jnp

def _softmax(x, axis=-1):
    return jax.nn.softmax(x, axis=axis)

def _gelu(x):
    return jax.nn.gelu(x, approximate=True)

def _silu(x):
    return jax.nn.silu(x)

def _sigmoid(x):
    return jax.nn.sigmoid(x)

def _layernorm(x, axis=-1, eps=1e-05):
    m = jnp.mean(x, axis=axis, keepdims=True)
    v = jnp.var(x, axis=axis, keepdims=True)
    return (x - m) / jnp.sqrt(v + eps)

def _scatter_add(tgt, idx, src, axis=0):
    return tgt.at[idx].add(src)

def _segment_sum(src, seg, n):
    return jax.ops.segment_sum(src, seg, n)
kernel_name = 'mk_gnn_resnorm_d4_gnn_r32_d251a2'

def setup_inputs(seed: int=0):
    np.random.seed(seed)
    _w = jnp.asarray

    def _rec_inputs():
        import jax
        import jax.numpy as jnp
        _gk = jax.random.key(seed)
        x = -0.0003713 + 1 * jax.random.normal(jax.random.fold_in(_gk, 1), (3125, 128), jnp.float32)
        _s = jax.random.randint(jax.random.fold_in(_gk, 2), (50000,), 0, 3125, jnp.int32)
        _d = jax.random.randint(jax.random.fold_in(_gk, 3), (50000,), 0, 3125, jnp.int32)
        _loop = jnp.arange(3125, dtype=jnp.int32)
        src = jnp.concatenate([_s, _d, _loop])
        dst = jnp.concatenate([_d, _s, _loop])
        _o = jnp.argsort(dst, stable=True)
        src = src[_o]
        dst = dst[_o]
        edge_attr_13 = 0.000262222 + 1.00012 * jax.random.normal(jax.random.fold_in(_gk, 12), (103125, 13), jnp.float32)
        edge_type_64 = jax.random.randint(jax.random.fold_in(_gk, 14), (103125,), 0, 64, jnp.int32)
        edge_weight1 = jax.random.uniform(jax.random.fold_in(_gk, 15), (103125, 1), jnp.float32, 0.0, 1)
        return (x, src, dst, edge_attr_13, edge_type_64, edge_weight1)
    x, src, dst, edge_attr_13, edge_type_64, edge_weight1 = _rec_inputs()

    def _L0_gnn_setup():
        import jax, jax.numpy as jnp
        import numpy as np
        N, E, IN, H, C, ED = (3125, 50000, 128, 4, 32, 13)
        NEG_SLOPE = 0.2
        LN_EPS = 1e-05
        key = jax.random.key(seed)
        ks = jax.random.split(key, 11)
        s = 0.05
        return {'x': jax.random.normal(ks[0], (N, IN), jnp.float32), 'edge_index': jax.random.randint(ks[1], (2, E), 0, N, jnp.int64), 'edge_attr': jax.random.normal(ks[2], (E, ED), jnp.float32), 'W': jax.random.normal(ks[3], (IN, H * C), jnp.float32) * s, 'att_src': jax.random.normal(ks[4], (H, C), jnp.float32) * s, 'att_dst': jax.random.normal(ks[5], (H, C), jnp.float32) * s, 'W_edge': jax.random.normal(ks[6], (ED, H * C), jnp.float32) * s, 'att_edge': jax.random.normal(ks[7], (H, C), jnp.float32) * s, 'bias': jax.random.normal(ks[8], (H * C,), jnp.float32) * s, 'ln_gamma': jnp.ones((H * C,), jnp.float32), 'ln_beta': jnp.zeros((H * C,), jnp.float32)}
    _L0_gnn_all = _L0_gnn_setup()
    _L0_gnn_in = {k: v for k, v in _L0_gnn_all.items() if k in ('W', 'att_src', 'att_dst', 'W_edge', 'att_edge', 'bias', 'ln_gamma', 'ln_beta')}
    del _L0_gnn_all

    def _L1_gnn_setup():
        import jax, jax.numpy as jnp
        import numpy as np
        N_NODES = 3125
        N_EDGES = 50000
        IN_FEAT = 128
        OUT_FEAT = 128
        NUM_RELS = 64
        NUM_BASES = 8
        key = jax.random.key(seed)
        ks = jax.random.split(key, 8)
        x = jax.random.normal(ks[0], (N_NODES, IN_FEAT), dtype=jnp.float32)
        norm = jax.random.uniform(ks[1], (N_EDGES, 1), dtype=jnp.float32)
        weight = jax.random.normal(ks[2], (NUM_BASES, IN_FEAT, OUT_FEAT), dtype=jnp.float32) * 0.05
        w_comp = jax.random.normal(ks[3], (NUM_RELS, NUM_BASES), dtype=jnp.float32) * 0.3
        h_bias = jnp.zeros((OUT_FEAT,), dtype=jnp.float32)
        loop_weight = jax.random.normal(ks[4], (IN_FEAT, OUT_FEAT), dtype=jnp.float32) * 0.05
        src = jax.random.randint(ks[5], (N_EDGES,), 0, N_NODES, dtype=jnp.int64)
        dst = jax.random.randint(ks[6], (N_EDGES,), 0, N_NODES, dtype=jnp.int64)
        etypes = jax.random.randint(ks[7], (N_EDGES,), 0, NUM_RELS, dtype=jnp.int64)
        return {'x': x, 'norm': norm, 'weight': weight, 'w_comp': w_comp, 'h_bias': h_bias, 'loop_weight': loop_weight, 'src': src, 'dst': dst, 'etypes': etypes}
    _L1_gnn_all = _L1_gnn_setup()
    _L1_gnn_in = {k: v for k, v in _L1_gnn_all.items() if k in ('weight', 'w_comp', 'h_bias', 'loop_weight')}
    del _L1_gnn_all

    def _L2_gnn_setup():
        import jax, jax.numpy as jnp
        import numpy as np
        N = 50000
        E = 37500
        IN_DIM = 128
        HID = 16
        HEADS1 = 8
        OUT_DIM = 128
        EPS = 1e-16

        def _linear_params(key, fan_in, fan_out):
            kw, kb = jax.random.split(key)
            s = 1.0 / np.sqrt(fan_in)
            W = jax.random.uniform(kw, (fan_in, fan_out), minval=-s, maxval=s, dtype=jnp.float32)
            b = jax.random.uniform(kb, (fan_out,), minval=-s, maxval=s, dtype=jnp.float32)
            return (W, b)

        def _transformer_conv(x, src, dst, Wq, bq, Wk, bk, Wv, bv, Ws, bs, heads, ch):
            n = x.shape[0]
            q = (x @ Wq + bq).reshape(n, heads, ch)
            k = (x @ Wk + bk).reshape(n, heads, ch)
            v = (x @ Wv + bv).reshape(n, heads, ch)
            alpha = jnp.einsum('ehc,ehc->eh', q[dst], k[src]) / np.sqrt(ch)
            m = jax.ops.segment_max(alpha, dst, num_segments=n)
            m = jnp.where(jnp.isfinite(m), m, 0.0)
            ea = jnp.exp(alpha - jax.lax.stop_gradient(m)[dst])
            denom = jax.ops.segment_sum(ea, dst, num_segments=n)
            attn = ea / (denom[dst] + EPS)
            out = jax.ops.segment_sum(attn[:, :, None] * v[src], dst, num_segments=n)
            return out.reshape(n, heads * ch) + (x @ Ws + bs)
        key = jax.random.key(seed)
        ks = jax.random.split(key, 10)
        x = jax.random.normal(ks[0], (N, IN_DIM), dtype=jnp.float32)
        edge_index = jax.random.randint(ks[1], (2, E), 0, N, dtype=jnp.int64)
        Wq1, bq1 = _linear_params(ks[2], IN_DIM, HEADS1 * HID)
        Wk1, bk1 = _linear_params(ks[3], IN_DIM, HEADS1 * HID)
        Wv1, bv1 = _linear_params(ks[4], IN_DIM, HEADS1 * HID)
        Ws1, bs1 = _linear_params(ks[5], IN_DIM, HEADS1 * HID)
        Wq2, bq2 = _linear_params(ks[6], HEADS1 * HID, OUT_DIM)
        Wk2, bk2 = _linear_params(ks[7], HEADS1 * HID, OUT_DIM)
        Wv2, bv2 = _linear_params(ks[8], HEADS1 * HID, OUT_DIM)
        Ws2, bs2 = _linear_params(ks[9], HEADS1 * HID, OUT_DIM)
        return dict(x=x, edge_index=edge_index, Wq1=Wq1, bq1=bq1, Wk1=Wk1, bk1=bk1, Wv1=Wv1, bv1=bv1, Ws1=Ws1, bs1=bs1, Wq2=Wq2, bq2=bq2, Wk2=Wk2, bk2=bk2, Wv2=Wv2, bv2=bv2, Ws2=Ws2, bs2=bs2)
    _L2_gnn_all = _L2_gnn_setup()
    _L2_gnn_in = {k: v for k, v in _L2_gnn_all.items() if k in ('Wq1', 'bq1', 'Wk1', 'bk1', 'Wv1', 'bv1', 'Ws1', 'bs1', 'Wq2', 'bq2', 'Wk2', 'bk2', 'Wv2', 'bv2', 'Ws2', 'bs2')}
    del _L2_gnn_all

    def _L3_gnn_setup():
        import jax, jax.numpy as jnp
        import numpy as np
        N_NODES, N_EDGES, D_IN, D_HID = (50000, 25000, 128, 128)

        def _gcn_conv(x, W, b, src, dst, n):
            h = x @ W
            loop = jnp.arange(n, dtype=src.dtype)
            s = jnp.concatenate([src, loop])
            d = jnp.concatenate([dst, loop])
            deg = jax.ops.segment_sum(jnp.ones_like(d, dtype=h.dtype), d, num_segments=n)
            dinv = jax.lax.rsqrt(deg)
            norm = dinv[s] * dinv[d]
            msg = norm[:, None] * h[s]
            out = jax.ops.segment_sum(msg, d, num_segments=n)
            return out + b
        key = jax.random.key(seed)
        k = jax.random.split(key, 6)
        x = jax.random.normal(k[0], (N_NODES, D_IN), dtype=jnp.float32)
        edge_index = jax.random.randint(k[1], (2, N_EDGES), 0, N_NODES, dtype=jnp.int64)
        W1 = jax.random.normal(k[2], (D_IN, D_HID), dtype=jnp.float32) * (1.0 / np.sqrt(D_IN))
        b1 = jnp.zeros((D_HID,), dtype=jnp.float32)
        W2 = jax.random.normal(k[3], (D_HID, D_HID), dtype=jnp.float32) * (1.0 / np.sqrt(D_HID))
        b2 = jnp.zeros((D_HID,), dtype=jnp.float32)
        return {'x': x, 'edge_index': edge_index, 'W1': W1, 'b1': b1, 'W2': W2, 'b2': b2}
    _L3_gnn_all = _L3_gnn_setup()
    _L3_gnn_in = {k: v for k, v in _L3_gnn_all.items() if k in ('W1', 'b1', 'W2', 'b2')}
    del _L3_gnn_all
    return {'x': x, 'src': src, 'dst': dst, 'edge_attr_13': edge_attr_13, 'edge_type_64': edge_type_64, 'edge_weight1': edge_weight1, 'L0_gnn_W': _L0_gnn_in['W'], 'L0_gnn_att_src': _L0_gnn_in['att_src'], 'L0_gnn_att_dst': _L0_gnn_in['att_dst'], 'L0_gnn_W_edge': _L0_gnn_in['W_edge'], 'L0_gnn_att_edge': _L0_gnn_in['att_edge'], 'L0_gnn_bias': _L0_gnn_in['bias'], 'L0_gnn_ln_gamma': _L0_gnn_in['ln_gamma'], 'L0_gnn_ln_beta': _L0_gnn_in['ln_beta'], 'L1_gnn_weight': _L1_gnn_in['weight'], 'L1_gnn_w_comp': _L1_gnn_in['w_comp'], 'L1_gnn_h_bias': _L1_gnn_in['h_bias'], 'L1_gnn_loop_weight': _L1_gnn_in['loop_weight'], 'L2_gnn_Wq1': _L2_gnn_in['Wq1'], 'L2_gnn_bq1': _L2_gnn_in['bq1'], 'L2_gnn_Wk1': _L2_gnn_in['Wk1'], 'L2_gnn_bk1': _L2_gnn_in['bk1'], 'L2_gnn_Wv1': _L2_gnn_in['Wv1'], 'L2_gnn_bv1': _L2_gnn_in['bv1'], 'L2_gnn_Ws1': _L2_gnn_in['Ws1'], 'L2_gnn_bs1': _L2_gnn_in['bs1'], 'L2_gnn_Wq2': _L2_gnn_in['Wq2'], 'L2_gnn_bq2': _L2_gnn_in['bq2'], 'L2_gnn_Wk2': _L2_gnn_in['Wk2'], 'L2_gnn_bk2': _L2_gnn_in['bk2'], 'L2_gnn_Wv2': _L2_gnn_in['Wv2'], 'L2_gnn_bv2': _L2_gnn_in['bv2'], 'L2_gnn_Ws2': _L2_gnn_in['Ws2'], 'L2_gnn_bs2': _L2_gnn_in['bs2'], 'L3_gnn_W1': _L3_gnn_in['W1'], 'L3_gnn_b1': _L3_gnn_in['b1'], 'L3_gnn_W2': _L3_gnn_in['W2'], 'L3_gnn_b2': _L3_gnn_in['b2']}

def reference(x, src, dst, edge_attr_13, edge_type_64, edge_weight1, L0_gnn_W, L0_gnn_att_src, L0_gnn_att_dst, L0_gnn_W_edge, L0_gnn_att_edge, L0_gnn_bias, L0_gnn_ln_gamma, L0_gnn_ln_beta, L1_gnn_weight, L1_gnn_w_comp, L1_gnn_h_bias, L1_gnn_loop_weight, L2_gnn_Wq1, L2_gnn_bq1, L2_gnn_Wk1, L2_gnn_bk1, L2_gnn_Wv1, L2_gnn_bv1, L2_gnn_Ws1, L2_gnn_bs1, L2_gnn_Wq2, L2_gnn_bq2, L2_gnn_Wk2, L2_gnn_bk2, L2_gnn_Wv2, L2_gnn_bv2, L2_gnn_Ws2, L2_gnn_bs2, L3_gnn_W1, L3_gnn_b1, L3_gnn_W2, L3_gnn_b2):
    import jax
    import jax.numpy as jnp

    def _L0_gnn_ref(x, edge_index, edge_attr, W, att_src, att_dst, W_edge, att_edge, bias, ln_gamma, ln_beta):
        import jax, jax.numpy as jnp
        import numpy as np
        N, E, IN, H, C, ED = (3125, 50000, 128, 4, 32, 13)
        NEG_SLOPE = 0.2
        LN_EPS = 1e-05
        n = x.shape[0]
        src, dst = (edge_index[0], edge_index[1])
        cnt = jax.ops.segment_sum(jnp.ones_like(src, x.dtype), dst, num_segments=n)
        ea_loop = jax.ops.segment_sum(edge_attr, dst, num_segments=n) / jnp.maximum(cnt, 1.0)[:, None]
        loop = jnp.arange(n, dtype=src.dtype)
        src_a = jnp.concatenate([src, loop])
        dst_a = jnp.concatenate([dst, loop])
        ea = jnp.concatenate([edge_attr, ea_loop], 0)
        h = (x @ W).reshape(n, H, C)
        a_src = jnp.einsum('nhc,hc->nh', h, att_src)
        a_dst = jnp.einsum('nhc,hc->nh', h, att_dst)
        e = (ea @ W_edge).reshape(-1, H, C)
        a_edge = jnp.einsum('ehc,hc->eh', e, att_edge)
        alpha = a_src[src_a] + a_dst[dst_a] + a_edge
        alpha = jnp.where(alpha > 0, alpha, NEG_SLOPE * alpha)
        amax = jax.ops.segment_max(alpha, dst_a, num_segments=n)
        alpha = jnp.exp(alpha - amax[dst_a])
        denom = jax.ops.segment_sum(alpha, dst_a, num_segments=n)
        alpha = alpha / (denom[dst_a] + 1e-16)
        out = jax.ops.segment_sum(alpha[:, :, None] * h[src_a], dst_a, num_segments=n)
        out = out.reshape(n, H * C) + bias
        y = out + x
        mu = jnp.mean(y, axis=-1, keepdims=True)
        var = jnp.mean((y - mu) ** 2, axis=-1, keepdims=True)
        y = (y - mu) / jnp.sqrt(var + LN_EPS) * ln_gamma + ln_beta
        return jax.nn.relu(y)

    def _L1_gnn_ref(x, norm, weight, w_comp, h_bias, loop_weight, src, dst, etypes):
        import jax, jax.numpy as jnp
        import numpy as np
        N_NODES = 3125
        N_EDGES = 50000
        IN_FEAT = 128
        OUT_FEAT = 128
        NUM_RELS = 64
        NUM_BASES = 8
        num_nodes = x.shape[0]
        num_bases = weight.shape[0]
        a = w_comp[etypes]
        z = x[src]
        msg = a[:, 0:1] * (z @ weight[0])
        for b in range(1, num_bases):
            msg = msg + a[:, b:b + 1] * (z @ weight[b])
        msg = msg * norm
        agg = jax.ops.segment_sum(msg, dst, num_segments=num_nodes)
        out = agg + h_bias + x @ loop_weight
        return jax.nn.relu(out)

    def _L2_gnn_ref(x, edge_index, Wq1, bq1, Wk1, bk1, Wv1, bv1, Ws1, bs1, Wq2, bq2, Wk2, bk2, Wv2, bv2, Ws2, bs2):
        import jax, jax.numpy as jnp
        import numpy as np
        N = 50000
        E = 37500
        IN_DIM = 128
        HID = 16
        HEADS1 = 8
        OUT_DIM = 128
        EPS = 1e-16

        def _linear_params(key, fan_in, fan_out):
            kw, kb = jax.random.split(key)
            s = 1.0 / np.sqrt(fan_in)
            W = jax.random.uniform(kw, (fan_in, fan_out), minval=-s, maxval=s, dtype=jnp.float32)
            b = jax.random.uniform(kb, (fan_out,), minval=-s, maxval=s, dtype=jnp.float32)
            return (W, b)

        def _transformer_conv(x, src, dst, Wq, bq, Wk, bk, Wv, bv, Ws, bs, heads, ch):
            n = x.shape[0]
            q = (x @ Wq + bq).reshape(n, heads, ch)
            k = (x @ Wk + bk).reshape(n, heads, ch)
            v = (x @ Wv + bv).reshape(n, heads, ch)
            alpha = jnp.einsum('ehc,ehc->eh', q[dst], k[src]) / np.sqrt(ch)
            m = jax.ops.segment_max(alpha, dst, num_segments=n)
            m = jnp.where(jnp.isfinite(m), m, 0.0)
            ea = jnp.exp(alpha - jax.lax.stop_gradient(m)[dst])
            denom = jax.ops.segment_sum(ea, dst, num_segments=n)
            attn = ea / (denom[dst] + EPS)
            out = jax.ops.segment_sum(attn[:, :, None] * v[src], dst, num_segments=n)
            return out.reshape(n, heads * ch) + (x @ Ws + bs)
        src, dst = (edge_index[0], edge_index[1])
        h = _transformer_conv(x, src, dst, Wq1, bq1, Wk1, bk1, Wv1, bv1, Ws1, bs1, HEADS1, HID)
        out = _transformer_conv(h, src, dst, Wq2, bq2, Wk2, bk2, Wv2, bv2, Ws2, bs2, 1, OUT_DIM)
        return out

    def _L3_gnn_ref(x, edge_index, W1, b1, W2, b2):
        import jax, jax.numpy as jnp
        import numpy as np
        N_NODES, N_EDGES, D_IN, D_HID = (50000, 25000, 128, 128)

        def _gcn_conv(x, W, b, src, dst, n):
            h = x @ W
            loop = jnp.arange(n, dtype=src.dtype)
            s = jnp.concatenate([src, loop])
            d = jnp.concatenate([dst, loop])
            deg = jax.ops.segment_sum(jnp.ones_like(d, dtype=h.dtype), d, num_segments=n)
            dinv = jax.lax.rsqrt(deg)
            norm = dinv[s] * dinv[d]
            msg = norm[:, None] * h[s]
            out = jax.ops.segment_sum(msg, d, num_segments=n)
            return out + b
        n = x.shape[0]
        src, dst = (edge_index[0], edge_index[1])
        h = jax.nn.relu(_gcn_conv(x, W1, b1, src, dst, n))
        z = _gcn_conv(h, W2, b2, src, dst, n)
        return z
    edge_index = jnp.stack([src, dst])
    x = _layernorm(x + _L0_gnn_ref(x, edge_index, edge_attr_13, L0_gnn_W, L0_gnn_att_src, L0_gnn_att_dst, L0_gnn_W_edge, L0_gnn_att_edge, L0_gnn_bias, L0_gnn_ln_gamma, L0_gnn_ln_beta), axis=-1)
    x = _layernorm(x + _L1_gnn_ref(x, edge_weight1, L1_gnn_weight, L1_gnn_w_comp, L1_gnn_h_bias, L1_gnn_loop_weight, src, dst, edge_type_64), axis=-1)
    x = _layernorm(x + _L2_gnn_ref(x, edge_index, L2_gnn_Wq1, L2_gnn_bq1, L2_gnn_Wk1, L2_gnn_bk1, L2_gnn_Wv1, L2_gnn_bv1, L2_gnn_Ws1, L2_gnn_bs1, L2_gnn_Wq2, L2_gnn_bq2, L2_gnn_Wk2, L2_gnn_bk2, L2_gnn_Wv2, L2_gnn_bv2, L2_gnn_Ws2, L2_gnn_bs2), axis=-1)
    x = _layernorm(x + _L3_gnn_ref(x, edge_index, L3_gnn_W1, L3_gnn_b1, L3_gnn_W2, L3_gnn_b2), axis=-1)
    return x

_drawn_inputs = setup_inputs


def setup_inputs(seed=0):
    import zlib

    import numpy as np

    out = dict(_drawn_inputs(seed))
    spreads = {'L0_gnn_ln_gamma': (1.0, 0.2),
     'L0_gnn_ln_beta': (0.0, 0.1),
     'L1_gnn_h_bias': (0.0, 0.1),
     'L3_gnn_b1': (0.0, 0.1),
     'L3_gnn_b2': (0.0, 0.1)}
    factors = {'edge_attr_13': 8.0,
     'L0_gnn_att_src': 6.24,
     'L0_gnn_att_dst': 200.0,
     'L0_gnn_W_edge': 8.0,
     'L0_gnn_att_edge': 8.0,
     'L2_gnn_Wq1': 2.788,
     'L2_gnn_bq1': 8.0,
     'L2_gnn_Wk1': 2.742,
     'L2_gnn_bk1': 200.0,
     'L2_gnn_Wq2': 7.268,
     'L2_gnn_bq2': 8.0,
     'L2_gnn_Wk2': 7.465,
     'L2_gnn_bk2': 200.0}
    for name, (base, spread) in spreads.items():
        noise = np.random.default_rng([zlib.crc32(name.encode()), seed]).standard_normal(out[name].shape)
        drawn = base * np.exp(spread * noise) if base else spread * noise
        out[name] = jnp.asarray(drawn.astype(out[name].dtype))
    for name, factor in factors.items():
        out[name] = (out[name] * factor).astype(out[name].dtype)
    return out
```

```python
from contextlib import ExitStack

import concourse.bass as bass
from concourse import mybir

ALU = mybir.AluOpType
ACT = mybir.ActivationFunctionType
AX = mybir.AxisListType
F32 = mybir.dt.float32
I32 = mybir.dt.int32

N = 3125
E = 103125
D = 128
BN = 121
NB = 26
NP = NB * BN
T = 33
CH = 128 * T
MORE = E // CH
SMAX = NB + MORE
BIG = 1.0e30
BATCH = [list(range(g, min(g + 4, T))) for g in range(0, T, 4)]
NG = len(BATCH)
EPS = 1e-5


def phase_semaphores(nc, ctx, name):
    own = []

    def clear():
        nc.clear_and_free_semaphores(own)
        nc.all_engine_barrier()

    ctx.callback(clear)

    def sem(n):
        own.append(nc.alloc_semaphore(name=name + n))
        return own[-1]

    return sem


def layernorm(nc, dve, act_sem, dve_sem, y, mean, var, tmp, count):
    inv = 1.0 / D
    nc.vector.tensor_reduce(mean[:], y[:], AX.X, ALU.add)
    dve.drain()
    nc.vector.tensor_scalar(mean[:], mean[:], inv, None, ALU.mult)
    dve.drain()
    nc.vector.tensor_tensor(y[:], y[:], mean[:].unsqueeze(2).broadcast_to([BN, NB, D]), ALU.subtract)
    dve.drain()
    nc.vector.tensor_tensor(tmp[:], y[:], y[:], ALU.mult)
    dve.drain()
    nc.vector.tensor_reduce(var[:], tmp[:], AX.X, ALU.add)
    dve.drain()
    nc.vector.tensor_scalar(var[:], var[:], inv, EPS, ALU.mult, ALU.add).then_inc(dve_sem, 1)
    dve.wait_ge(act_sem, count)
    nc.vector.reciprocal(var[:], var[:])
    dve.drain()
    nc.vector.tensor_tensor(y[:], y[:], var[:].unsqueeze(2).broadcast_to([BN, NB, D]), ALU.mult)
    dve.drain()


def build(nc, a, out):
    with ExitStack() as top:
        def keep(name, shape, dt=F32):
            return top.enter_context(nc.sbuf_tensor(name, shape, dt))

        X = keep("X", [BN, NB, D])
        RES = keep("RES", [BN, NB, 152])
        Q = keep("Q", [BN, NB, D])
        SKIP = keep("SKIP", [BN, NB, D])
        eye = keep("eye", [128, 128])
        iota = keep("iota", [128, 128])
        pidx = keep("pidx", [128, 1])
        base_t = keep("base_t", [128, SMAX])
        basep_t = keep("basep_t", [128, SMAX])
        neg_t = keep("neg_t", [128, SMAX])
        keep_t = keep("keep_t", [128, SMAX])
        steps_i = keep("steps_i", [1, 2 * SMAX + 2], I32)
        cnt1 = keep("cnt1", [BN, NB])

        tab = {w: nc.dram_tensor(f"table_{w}", [NP, w], F32).ap() for w in (132, 128, 256)}

        def n_steps(eng):
            return eng.value_load(steps_i[0:1, 2 * SMAX:2 * SMAX + 1], min_val=NB, max_val=SMAX)

        plan_steps(nc, a, X, eye, iota, pidx, base_t, basep_t, neg_t, keep_t, steps_i)
        g = dict(iota_p=pidx, nc=nc, a=a, X=X, RES=RES, Q=Q, SKIP=SKIP, eye=eye, iota=iota, base_t=base_t,
                 basep_t=basep_t, neg_t=neg_t, keep_t=keep_t, steps_i=steps_i, n_steps=n_steps, cnt1=cnt1)

        project(g, "p0", [("L0_gnn_W", None, 0.0)], tab[132], "gat")
        attention_pass(g, "e0", tab[132], 132, 4, True)
        gat_finish(g)
        project(g, "p1", [], tab[128], "copy")
        relation_pass(g, "e1", tab[128])
        relation_finish(g)
        for c, heads in ((1, 8), (2, 1)):
            ws = [(f"L2_gnn_W{n}{c}", f"L2_gnn_b{n}{c}", 0.0) for n in "kvqs"]
            if c == 2:
                src = RES
            project(g, f"p2{c}", ws, tab[256], "qkv", scale=float(D // heads) ** -0.5, source=X if c == 1 else RES)
            attention_pass(g, f"e2{c}", tab[256], 256, heads, False)
            transformer_finish(g, f"f2{c}", heads, last=(c == 2))
        for c in (1, 2):
            project(g, f"p3{c}", [(f"L3_gnn_W{c}", None, 0.0)], tab[128], "gcn", source=X if c == 1 else RES)
            sum_pass(g, f"e3{c}", tab[128])
            gcn_finish(g, f"f3{c}", f"L3_gnn_b{c}", out if c == 2 else None)


def plan_steps(nc, a, X, eye, iota, pidx, base_t, basep_t, neg_t, keep_t, steps_i):
    PF = E // 128 + 1
    with ExitStack() as ctx:
        sb = lambda n, s, dt=F32: ctx.enter_context(nc.sbuf_tensor(n, s, dt))
        sem = phase_semaphores(nc, ctx, "plan")
        dsti = sb("dsti", [128, PF], I32)
        below = sb("below", [128, PF])
        part = sb("part", [128, NB + 1])
        ones = sb("ones", [128, 128])
        cum = sb("cum", [1, NB + 1])
        cnt = sb("cnt", [1, NB])
        nst = sb("nst", [1, NB])
        endn = sb("endn", [1, NB])
        zero = sb("zero", [1, NB])
        big1 = sb("big1", [1, NB, MORE])
        past = sb("past", [1, SMAX, NB])
        prod = sb("prod", [1, SMAX, NB])
        row = sb("row", [1, 6, SMAX])
        ch = sb("ch", [1, MORE])
        ps = ctx.enter_context(nc.psum_tensor("ps_plan", [128, 512], F32))
        ps2 = ctx.enter_context(nc.psum_tensor("ps_plan2", [128, 512], F32))
        loaded, counted, summed, ready, spread = (sem(n) for n in ("loaded", "counted", "summed", "ready", "spread"))
        block = ctx.enter_context(nc.Block())

        @block.sync
        def _(sp):
            sp.dma_start(dsti[:], a["dst_rows"]).then_inc(loaded, 16)
            sp.dma_start(X[:], a["x"].rearrange("(b p) f -> p b f", p=BN)).then_inc(loaded, 16)
            sp.dma_start(eye[:], a["eye"]).then_inc(loaded, 16)
            sp.dma_start(iota[:], a["iota"].partition_broadcast(128)).then_inc(loaded, 16)
            sp.dma_start(pidx[:], a["iota"].rearrange("(p a) -> p a", a=1)).then_inc(loaded, 16)
            sp.dma_start(ch[:], a["more"].rearrange("(a p) -> a p", a=1)).then_inc(loaded, 16)

        @block.vector
        def _(dve):
            dve.wait_ge(loaded, 96)
            nc.vector.memset(ones[:], 1.0)
            nc.vector.memset(zero[:], 0.0)
            for b in range(NB + 1):
                nc.vector.tensor_scalar(below[:], dsti[:], float(b * BN) if b < NB else float(NP), None, ALU.is_lt)
                dve.drain()
                nc.vector.tensor_reduce(part[:, b:b + 1], below[:], AX.X, ALU.add)
                dve.drain()
            nc.vector.memset(row[:], 0.0).then_inc(counted, 1)
            dve.wait_ge(summed, 1)
            nc.vector.tensor_copy(cum[:], ps[0:1, 0:NB + 1])
            dve.drain()
            nc.vector.tensor_tensor(cnt[:], cum[:, 1:NB + 1], cum[:, 0:NB], ALU.subtract)
            dve.drain()
            nc.vector.tensor_tensor(big1[:], cnt[:].unsqueeze(2).broadcast_to([1, NB, MORE]),
                                    ch[:].unsqueeze(1).broadcast_to([1, NB, MORE]), ALU.is_gt)
            dve.drain()
            nc.vector.tensor_reduce(nst[:], big1[:], AX.X, ALU.add)
            dve.drain()
            nc.vector.tensor_scalar(nst[:], nst[:], 1.0, None, ALU.add)
            dve.drain()
            nc.vector.tensor_tensor_scan(endn[:], nst[:], zero[:], 0.0, ALU.add, ALU.add)
            dve.drain()
            nc.vector.tensor_tensor(past[:], endn[:].unsqueeze(1).broadcast_to([1, SMAX, NB]),
                                    iota[0:1, 0:SMAX].unsqueeze(2).broadcast_to([1, SMAX, NB]), ALU.is_le)
            dve.drain()
            nc.vector.tensor_reduce(row[:, 0, :], past[:], AX.X, ALU.add)
            for k, v in ((1, cnt), (2, nst)):
                nc.vector.tensor_tensor(prod[:], past[:], v[:].unsqueeze(1).broadcast_to([1, SMAX, NB]), ALU.mult)
                dve.drain()
                nc.vector.tensor_reduce(row[:, k, :], prod[:], AX.X, ALU.add)
                dve.drain()
            nc.vector.tensor_tensor(row[:, 2, :], iota[0:1, 0:SMAX], row[:, 2, :], ALU.subtract)
            dve.drain()
            nc.vector.scalar_tensor_tensor(out=row[:, 1, :], in0=row[:, 2, :], scalar=float(CH), in1=row[:, 1, :],
                                           op0=ALU.mult, op1=ALU.add)
            nc.vector.tensor_scalar(row[:, 3, :], row[:, 2, :], 0.0, None, ALU.is_equal)
            dve.drain()
            nc.vector.tensor_scalar(row[:, 4, :], row[:, 3, :], -BIG, None, ALU.mult)
            nc.vector.tensor_scalar(row[:, 5, :], row[:, 3, :], -1.0, 1.0, ALU.mult, ALU.add)
            dve.drain()
            nc.vector.tensor_scalar(row[:, 3, :], row[:, 0, :], float(BN), None, ALU.mult)
            nc.vector.tensor_scalar(row[:, 0, :], row[:, 0, :], float(NB - 1), None, ALU.min)
            nc.vector.tensor_scalar(row[:, 1, :], row[:, 1, :], float(E), None, ALU.min)
            dve.drain()
            nc.vector.tensor_copy(steps_i[:, 0:SMAX], row[:, 0, :])
            nc.vector.tensor_copy(steps_i[:, SMAX:2 * SMAX], row[:, 1, :])
            nc.vector.tensor_copy(steps_i[:, 2 * SMAX:2 * SMAX + 1], endn[:, NB - 1:NB])
            dve.drain()
            nc.vector.memset(zero[:], 0.0).then_inc(ready, 1)
            dve.wait_ge(spread, 1)
            nc.vector.tensor_copy(base_t[:], ps2[:, 0:SMAX])
            nc.vector.tensor_scalar(basep_t[:], ps2[:, 0:SMAX], pidx[:, 0:1], None, ALU.add)
            nc.vector.tensor_copy(neg_t[:], ps2[:, SMAX:2 * SMAX])
            nc.vector.tensor_copy(keep_t[:], ps2[:, 2 * SMAX:3 * SMAX])
            dve.drain()

        @block.tensor
        def _(pe):
            pe.wait_ge(counted, 1)
            nc.tensor.matmul(ps[0:1, 0:NB + 1], ones[:, 0:1], part[:], start=True, stop=True).then_inc(summed, 1)
            pe.wait_ge(ready, 1)
            nc.tensor.matmul(ps2[:, 0:3 * SMAX], ones[0:1, :], row[:, 3:6, :], start=True, stop=True).then_inc(spread, 1)


def project(g, name, weights, table, kind, scale=1.0, source=None):
    nc, a, X, RES, Q, SKIP, eye, cnt1 = (g[k] for k in ("nc", "a", "X", "RES", "Q", "SKIP", "eye", "cnt1"))
    source = source or X
    W = D * len(weights)
    width = table.shape[1]
    with ExitStack() as ctx:
        sb = lambda n, s, dt=F32: ctx.enter_context(nc.sbuf_tensor(name + n, s, dt))
        sem = phase_semaphores(nc, ctx, name)
        if kind == "copy":
            stored = sem("stored")
            block = ctx.enter_context(nc.Block())

            @block.sync
            def _(sp):
                sp.dma_start(table.rearrange("(b p) f -> p b f", p=BN), source[:, :, 0:D]).then_inc(stored, 16)
                sp.wait_ge(stored, 16)
            return
        w = sb("w", [D, W])
        bias = sb("bias", [BN, W])
        xT = sb("xT", [D, 2, BN])
        rows = sb("rows", [BN, NB, width])
        att = sb("att", [BN, 2, D])
        tmp = sb("tmp", [BN, NB, D])
        psT = ctx.enter_context(nc.psum_tensor(name + "psT", [128, 2, 512], F32))
        psY = ctx.enter_context(nc.psum_tensor(name + "psY", [128, 2, 512], F32))
        loaded, turned, copied, made, used, stored, rooted = (
            sem(n) for n in ("loaded", "turned", "copied", "made", "used", "stored", "rooted"))
        n_loads = len(weights) + sum(b is not None for _, b, _ in weights) + 2 * (kind == "gat")
        block = ctx.enter_context(nc.Block())

        @block.sync
        def _(sp):
            for i, (wn, bn, _) in enumerate(weights):
                sp.dma_start(w[:, i * D:(i + 1) * D], a[wn]).then_inc(loaded, 16)
                if bn:
                    sp.dma_start(bias[:, i * D:(i + 1) * D], a[bn].partition_broadcast(BN)).then_inc(loaded, 16)
            if kind == "gat":
                for i, n in enumerate(("L0_gnn_att_src", "L0_gnn_att_dst")):
                    sp.dma_start(att[:, i, :], a[n].rearrange("h c -> (h c)").partition_broadcast(BN)).then_inc(loaded, 16)
            sp.wait_ge(used, NB + 1)
            sp.dma_start(table.rearrange("(b p) f -> p b f", p=BN), rows[:]).then_inc(stored, 16)
            sp.wait_ge(stored, 16)

        @block.tensor
        def _(pe):
            pe.wait_ge(loaded, 16 * n_loads)
            for b in range(NB + 1):
                if b < NB:
                    if b >= 2:
                        pe.wait_ge(copied, b - 1)
                    nc.tensor.transpose(psT[:, b % 2, 0:BN], source[:, b, 0:D], eye[0:BN, 0:BN]).then_inc(turned, 1)
                if b >= 1:
                    c = b - 1
                    pe.wait_ge(copied, c + 1)
                    if c >= 2:
                        pe.wait_ge(used, c - 1)
                    nc.tensor.matmul(psY[0:BN, c % 2, 0:W], xT[:, c % 2, :], w[:], start=True, stop=True).then_inc(made, 1)

        @block.scalar
        def _(act):
            for b in range(NB):
                act.wait_ge(turned, b + 1)
                if b >= 2:
                    act.wait_ge(made, b - 1)
                nc.scalar.copy(xT[:, b % 2, :], psT[:, b % 2, 0:BN]).then_inc(copied, 1)
            if kind == "gcn":
                act.wait_ge(used, NB)
                act.wait_ge(stored, 0) if False else None

        @block.vector
        def _(dve):
            dve.wait_ge(loaded, 16 * n_loads)
            for b in range(NB):
                dve.wait_ge(made, b + 1)
                if kind == "gat":
                    nc.vector.tensor_copy(rows[:, b, 4:4 + D], psY[0:BN, b % 2, 0:D]).then_inc(used, 1)
                elif kind == "gcn":
                    nc.vector.tensor_scalar(rows[:, b, :], psY[0:BN, b % 2, 0:D], cnt1[:, b:b + 1], None,
                                            ALU.mult).then_inc(used, 1)
                else:
                    nc.vector.tensor_tensor(rows[:, b, :], psY[0:BN, b % 2, 0:2 * D], bias[:, 0:2 * D], ALU.add)
                    nc.vector.tensor_tensor(Q[:, b, :], psY[0:BN, b % 2, 2 * D:3 * D], bias[:, 2 * D:3 * D], ALU.add)
                    nc.vector.tensor_tensor(SKIP[:, b, :], psY[0:BN, b % 2, 3 * D:4 * D], bias[:, 3 * D:4 * D],
                                            ALU.add).then_inc(used, 1)
            dve.drain()
            if kind == "gat":
                h = rows[:, :, 4:4 + D]
                for i in range(2):
                    nc.vector.tensor_tensor(tmp[:], h, att[:, i:i + 1, :].broadcast_to([BN, NB, D]), ALU.mult)
                    dve.drain()
                    dst = rows[:, :, 0:4] if i == 0 else Q[:, :, 0:4]
                    nc.vector.tensor_reduce(dst, tmp[:].rearrange("p b (h c) -> p b h c", h=4), AX.X, ALU.add)
                    dve.drain()
                nc.vector.tensor_copy(SKIP[:], h)
                nc.vector.tensor_copy(Q[:, :, 4:8], rows[:, :, 0:4])
            if kind == "qkv":
                nc.vector.tensor_scalar(Q[:], Q[:], scale, None, ALU.mult)
            if kind == "gcn":
                nc.vector.tensor_copy(SKIP[:], rows[:])
            dve.drain()
            nc.vector.memset(bias[:, 0:1], 0.0).then_inc(used, 1)


def load_steps(nc, sp, g, a, buffers, first, later):
    steps_i = g["steps_i"]
    done, sems = later

    def issue(s):
        e = sp.value_load(steps_i[0:1, bass.ds(s + SMAX, 1)], min_val=0, max_val=E)
        for buf, name in buffers:
            if name == "src_p":
                sp.dma_start(buf[:], a[name][bass.ds(e, CH)].rearrange("(p t) -> p t", p=128)).then_inc(first, 16)
            elif name == "dst_p":
                w = a[name][bass.ds(e, CH + 2)]
                w = bass.AP(w.tensor, w.offset, [[T, 128], [1, T + 2]])
                sp.dma_start(buf[:], w).then_inc(first, 16)
            elif name == "dst_all":
                sp.dma_start(buf[:], a["dst_p"][bass.ds(e + 1, CH)].partition_broadcast(BN)).then_inc(first, 16)
            elif name == "type_p":
                sp.dma_start(buf[:], a[name][bass.ds(e, CH)].partition_broadcast(64)).then_inc(first, 16)
            elif name == "weight_p":
                sp.dma_start(buf[:], a[name][bass.ds(e, CH)].rearrange("(p t) -> p t", p=128)).then_inc(first, 16)
            else:
                sp.dma_start(buf[:], a[name][bass.ds(e, CH), :].rearrange("(p t) c -> p (t c)", p=128)).then_inc(first, 16)

    issue(0)
    with sp.Fori(1, g["n_steps"](sp)) as s:
        for sem, each in sems:
            sp.wait_ge(sem, s * each)
        issue(s)


def attention_pass(g, name, table, width, H, gat):
    nc, a, RES, Q = (g[k] for k in ("nc", "a", "RES", "Q"))
    C = D // H
    vo = width - D
    wo, mo, fo = width, width + H, width + 2 * H
    extra = 5 if gat else 0
    GW = fo + 1 + extra
    NC = D + 2 * H + 1 + extra
    QW = 4 if gat else D
    with ExitStack() as ctx:
        sb = lambda n, s, dt=F32: ctx.enter_context(nc.sbuf_tensor(name + n, s, dt))
        sem = phase_semaphores(nc, ctx, name)
        G = sb("G", [128, T, GW])
        src = sb("src", [128, T], I32)
        dst3 = sb("dst3", [128, T + 2], I32)
        dstb = sb("dstb", [BN, CH], I32)
        dstf = sb("dstf", [128, T + 2])
        OT = sb("OT", [BN, CH])
        O = sb("O", [128, T, BN])
        ne = sb("ne", [128, T + 1])
        rb = sb("rb", [128, T + 1])
        hm = sb("hm", [128, T])
        tm = sb("tm", [128, T])
        Rf = sb("Rf", [128, H, T])
        Rb = sb("Rb", [128, H, T])
        A = sb("A", [128, H, T])
        Fw = sb("Fw", [128, H, T])
        M = sb("M", [128, H, T])
        X1 = sb("X1", [128, H, T])
        TI = sb("TI", [128, 6, H])
        TS = sb("TS", [H, 6, 128])
        UV = sb("UV", [H, 2, 128])
        LR = sb("LR", [H, 2, 128])
        ST = sb("ST", [BN, NC])
        acc = sb("acc", [BN, NC])
        mm = sb("mm", [BN, 3 * H])
        ex = sb("ex", [BN, 2 * H])
        if gat:
            attr = sb("attr", [128, T, 13], F32)
            wed = sb("wed", [128, 13, D])
            atte = sb("atte", [128, D])
            we = sb("we", [128, 4, 13])
            pr = sb("pr", [128, T, 13])
        psQ = ctx.enter_context(nc.psum_tensor(name + "psQ", [128, 3, 512], F32))
        psA = ctx.enter_context(nc.psum_tensor(name + "psA", [128, 512], F32))
        psT = ctx.enter_context(nc.psum_tensor(name + "psT", [128, 2, 512], F32))
        psB = ctx.enter_context(nc.psum_tensor(name + "psB", [128, 512], F32))
        names = ("waited", "edges_in", "edges_used", "slots_free", "spread_ready", "spread_free", "targets_ready", "ends_ready",
                 "ends_turned", "carry_ready", "carry_turned", "diff_ready", "weights_done", "values_ready",
                 "sums_done", "sums_free", "merge_ready", "merge_done", "pe_waited", "consts")
        S = {n: sem(n) for n in names}
        gathered = [sem(f"gathered{b}") for b in range(NG)]
        n_in = 4 if gat else 3
        block = ctx.enter_context(nc.Block())

        @block.sync
        def _(sp):
            if gat:
                sp.dma_start(wed[:].rearrange("p a f -> p (a f)"), a["L0_gnn_W_edge"].rearrange("a f -> (a f)").partition_broadcast(128)).then_inc(S["consts"], 16)
                sp.dma_start(atte[:], a["L0_gnn_att_edge"].rearrange("h c -> (h c)").partition_broadcast(128)).then_inc(S["consts"], 16)
            bufs = [(src, "src_p"), (dst3, "dst_p"), (dstb, "dst_all")]
            if gat:
                bufs.append((attr[:].rearrange("p t c -> p (t c)"), "attr_p"))
            load_steps(nc, sp, g, a, bufs, S["edges_in"],
                       (None, [(gathered[-1], 16 * len(BATCH[-1])), (S["edges_used"], 1)]))

        @block.gpsimd
        def _(pool):
            with pool.Fori(0, g["n_steps"](pool)) as s:
                pool.wait_ge(S["edges_in"], s * (16 * n_in) + 16 * n_in)
                for b, tiles in enumerate(BATCH):
                    pool.wait_ge(S["slots_free"], s * NG + b + 1)
                    pool.sem_inc(S["waited"], 1)
                    for t in tiles:
                        nc.gpsimd.indirect_dma_start(
                            out=G[:, t, 0:width], out_offset=None, in_=table,
                            in_offset=bass.IndirectOffsetOnAxis(ap=src[:, t:t + 1], axis=0)).then_inc(gathered[b], 16)

        @block.tensor
        def _(pe):
            pe.sem_inc(S["slots_free"], NG)
            with pe.Fori(0, g["n_steps"](pe)) as s:
                blk = pe.value_load(g["steps_i"][0:1, bass.ds(s, 1)], min_val=0, max_val=NB - 1)
                pe.wait_ge(S["targets_ready"], s + 1)
                onehot = OT[:].rearrange("d (p t) -> d t p", t=T)
                for b, tiles in enumerate(BATCH):
                    pe.wait_ge(S["spread_free"], s * NG + b + 1)
                    for i, t in enumerate(tiles):
                        mmi = nc.tensor.matmul(psQ[:, b % 3, i * QW:(i + 1) * QW], onehot[:, t, :],
                                               Q[:, bass.ds(blk, 1), 0:QW].rearrange("p a f -> p (a f)"), start=True, stop=True)
                    mmi.then_inc(S["spread_ready"], 1)
                pe.wait_ge(S["ends_ready"], s + 1)
                for k in range(6):
                    mmi = nc.tensor.transpose(psT[0:H, k // 4, (k % 4) * 128:(k % 4 + 1) * 128], TI[:, k, :], g["eye"][:])
                mmi.then_inc(S["ends_turned"], 1)
                pe.wait_ge(S["carry_ready"], s + 1)
                pe.sem_inc(S["pe_waited"], 1)
                for k in range(2):
                    mmi = nc.tensor.transpose(psB[:, k * H:(k + 1) * H], LR[:, k, :], g["eye"][0:H, 0:H])
                mmi.then_inc(S["carry_turned"], 1)
                pe.wait_ge(S["sums_free"], s + 1)
                for b, tiles in enumerate(BATCH):
                    pe.wait_ge(S["values_ready"], s * NG + b + 1)
                    for t in tiles:
                        mmi = nc.tensor.matmul(psA[0:BN, 0:NC], O[:, t, :], G[:, t, vo:vo + NC],
                                               start=(t == 0), stop=(t == T - 1))
                    if b < NG - 1:
                        mmi.then_inc(S["slots_free"], 1)
                mmi.then_inc(S["sums_done"], 1)
                pe.wait_ge(S["sums_done"], s + 1)
                pe.sem_inc(S["slots_free"], 1)

        @block.scalar
        def _(act):
            with act.Fori(0, g["n_steps"](act)) as s:
                act.wait_ge(S["diff_ready"], s + 1)
                nc.scalar.activation(G[:, :, wo:wo + H].rearrange("p t h -> p h t"), A[:], ACT.Exp).then_inc(S["weights_done"], 1)
                act.wait_ge(S["merge_ready"], s + 1)
                nc.scalar.activation(ex[:], mm[:, 0:2 * H], ACT.Exp).then_inc(S["merge_done"], 1)

        @block.vector
        def _(dve):
            def bc(x, shape):
                return x.broadcast_to(shape)

            V = nc.vector
            if gat:
                dve.wait_ge(S["consts"], 32)
                V.tensor_tensor(wed[:], wed[:], bc(atte[:].unsqueeze(1), [128, 13, D]), ALU.mult)
                dve.drain()
                V.tensor_reduce(we[:].rearrange("p h k -> p k h"), wed[:].rearrange("p k (h c) -> p k h c", h=4), AX.X, ALU.add)
                V.memset(G[:, :, GW - 1:GW], 1.0)
            V.memset(ST[:], 0.0)
            V.memset(LR[:], -BIG)
            V.memset(Rf[:, :, 0:1], -BIG)
            V.memset(Rb[:, :, T - 1:T], -BIG)
            dve.drain()
            dve.sem_inc(S["spread_free"], 3)
            dve.sem_inc(S["sums_free"], 1)
            with dve.Fori(0, g["n_steps"](dve)) as s:
                blk = dve.value_load(g["steps_i"][0:1, bass.ds(s, 1)], min_val=0, max_val=NB - 1)
                sc = bass.ds(s, 1)
                dve.wait_ge(S["edges_in"], s * (16 * n_in) + 16 * n_in)
                V.tensor_scalar(dstf[:], dst3[:], g["base_t"][:, sc], None, ALU.subtract)
                V.tensor_scalar(OT[:], dstb[:], g["basep_t"][0:BN, sc], None, ALU.is_equal)
                dve.drain()
                V.tensor_tensor(O[:], bc(g["iota"][:, 0:BN].unsqueeze(1), [128, T, BN]),
                                bc(dstf[:, 1:T + 1].unsqueeze(2), [128, T, BN]), ALU.is_equal).then_inc(S["targets_ready"], 1)
                V.tensor_tensor(ne[:], dstf[:, 1:T + 2], dstf[:, 0:T + 1], ALU.not_equal)
                V.tensor_scalar(hm[:], dstf[:, 1:T + 1], dstf[:, 1:2], -BIG, ALU.not_equal, ALU.mult)
                V.tensor_scalar(tm[:], dstf[:, 1:T + 1], dstf[:, T:T + 1], -BIG, ALU.not_equal, ALU.mult)
                dve.drain()
                V.memset(ne[0:1, 0:1], 1.0)
                dve.drain()
                V.tensor_scalar(rb[:], ne[:], -BIG, None, ALU.mult)
                dve.drain()
                V.tensor_copy(Rf[:, :, 1:T], bc(rb[:, 1:T].unsqueeze(1), [128, H, T - 1]))
                V.tensor_copy(Rb[:, :, 0:T - 1], bc(rb[:, 1:T].unsqueeze(1), [128, H, T - 1]))
                if gat:
                    for h in range(4):
                        V.tensor_tensor(pr[:], attr[:], bc(we[:, h:h + 1, :], [128, T, 13]), ALU.mult)
                        dve.drain()
                        V.tensor_reduce(G[:, :, GW - 5 + h:GW - 4 + h].rearrange("p t a -> p (t a)"), pr[:], AX.X, ALU.add)
                        dve.drain()
                V.memset(X1[:], 0.0).then_inc(S["edges_used"], 1)
                for b, tiles in enumerate(BATCH):
                    n = len(tiles)
                    t0, t1 = tiles[0], tiles[-1] + 1
                    dve.wait_ge(gathered[b], s * (16 * n) + 16 * n)
                    dve.wait_ge(S["spread_ready"], s * NG + b + 1)
                    q = psQ[:, b % 3, 0:n * QW].rearrange("p (t f) -> p t f", f=QW)
                    if gat:
                        V.tensor_tensor(A[:, :, t0:t1].rearrange("p h t -> p t h"), q, G[:, t0:t1, 0:4], ALU.add).then_inc(S["spread_free"], 1)
                    else:
                        V.tensor_tensor(G[:, t0:t1, 0:D], q, G[:, t0:t1, 0:D], ALU.mult).then_inc(S["spread_free"], 1)
                        dve.drain()
                        V.tensor_reduce(A[:, :, t0:t1].rearrange("p h t -> p t h"),
                                        G[:, t0:t1, 0:D].rearrange("p t (h c) -> p t h c", h=H), AX.X, ALU.add)
                dve.drain()
                if gat:
                    V.tensor_tensor(A[:], A[:], G[:, :, GW - 5:GW - 1].rearrange("p t h -> p h t"), ALU.add)
                    dve.drain()
                    V.scalar_tensor_tensor(out=A[:], in0=A[:], scalar=0.2, in1=A[:], op0=ALU.mult, op1=ALU.max)
                    dve.drain()
                fl = lambda x: x[:].rearrange("p h t -> p (h t)")
                V.tensor_tensor_scan(fl(Fw), fl(Rf), fl(A), -BIG, ALU.add, ALU.max)
                dve.drain()
                V.tensor_tensor_scan(fl(M)[:, ::-1], fl(Rb)[:, ::-1], fl(Fw)[:, ::-1], -BIG, ALU.add, ALU.max)
                dve.drain()
                V.tensor_copy(TI[:, 0, :], Fw[:, :, T - 1])
                V.tensor_copy(TI[:, 1, :], M[:, :, 0])
                V.tensor_tensor(TI[:, 2, :], bc(hm[:, T - 1:T], [128, H]), bc(rb[:, 0:1], [128, H]), ALU.min)
                V.tensor_tensor(TI[:, 3, :], bc(hm[:, T - 1:T], [128, H]), bc(rb[:, T:T + 1], [128, H]), ALU.min)
                V.tensor_copy(TI[:, 4, :], bc(rb[:, 0:1], [128, H]))
                V.tensor_copy(TI[:, 5, :], bc(rb[:, T:T + 1], [128, H])).then_inc(S["ends_ready"], 1)
                dve.wait_ge(S["ends_turned"], s + 1)
                V.tensor_copy(TS[:].rearrange("h k p -> h (k p)"), psT[0:H, :, :].rearrange("h a b -> h (a b)")[:, 0:768])
                dve.drain()
                V.tensor_tensor_scan(UV[:, 0, :], TS[:, 2, :], TS[:, 0, :], -BIG, ALU.add, ALU.max)
                V.tensor_tensor_scan(UV[:, 1, ::-1], TS[:, 3, ::-1], TS[:, 1, ::-1], -BIG, ALU.add, ALU.max)
                dve.drain()
                V.tensor_tensor(LR[:, 0, 1:128], UV[:, 0, 0:127], TS[:, 4, 1:128], ALU.add)
                V.tensor_tensor(LR[:, 1, 0:127], UV[:, 1, 1:128], TS[:, 5, 0:127], ALU.add).then_inc(S["carry_ready"], 1)
                dve.wait_ge(S["carry_turned"], s + 1)
                for k, mask in ((0, hm), (1, tm)):
                    V.tensor_tensor(X1[:], bc(psB[:, k * H:(k + 1) * H].unsqueeze(2), [128, H, T]),
                                    bc(mask[:].unsqueeze(1), [128, H, T]), ALU.add)
                    dve.drain()
                    V.tensor_tensor(M[:], M[:], X1[:], ALU.max)
                    dve.drain()
                V.tensor_tensor(A[:], A[:], M[:], ALU.subtract).then_inc(S["diff_ready"], 1)
                V.tensor_tensor(G[:, :, mo:mo + H].rearrange("p t h -> p h t"), M[:], bc(ne[:, 0:T].unsqueeze(1), [128, H, T]), ALU.mult)
                V.tensor_copy(G[:, :, fo:fo + 1].rearrange("p t a -> p (t a)"), ne[:, 0:T])
                dve.wait_ge(S["weights_done"], s + 1)
                for b, tiles in enumerate(BATCH):
                    t0, t1 = tiles[0], tiles[-1] + 1
                    v = G[:, t0:t1, vo:vo + D].rearrange("p t (h c) -> p t h c", h=H)
                    V.tensor_tensor(v, v, bc(G[:, t0:t1, wo:wo + H].unsqueeze(3), [128, t1 - t0, H, C]), ALU.mult).then_inc(S["values_ready"], 1)
                dve.wait_ge(S["sums_done"], s + 1)
                V.tensor_copy(acc[:], psA[0:BN, 0:NC]).then_inc(S["sums_free"], 1)
                dve.drain()
                V.tensor_scalar(mm[:, 2 * H:2 * H + 1], acc[:, D + 2 * H:D + 2 * H + 1], BIG, -BIG, ALU.mult, ALU.add)
                dve.drain()
                V.tensor_scalar(mm[:, H:2 * H], acc[:, D + H:D + 2 * H], mm[:, 2 * H:2 * H + 1], None, ALU.add)
                V.tensor_scalar(mm[:, 0:H], ST[:, D + H:D + 2 * H], g["neg_t"][0:BN, sc], None, ALU.add)
                dve.drain()
                V.tensor_tensor(ST[:, D + H:D + 2 * H], mm[:, 0:H], mm[:, H:2 * H], ALU.max)
                dve.drain()
                V.tensor_tensor(mm[:, 0:2 * H].rearrange("p (k h) -> p k h", k=2), mm[:, 0:2 * H].rearrange("p (k h) -> p k h", k=2),
                                bc(ST[:, D + H:D + 2 * H].unsqueeze(1), [BN, 2, H]), ALU.subtract).then_inc(S["merge_ready"], 1)
                dve.wait_ge(S["merge_done"], s + 1)
                for x, k in ((ST, 0), (acc, 1)):
                    xv = x[:, 0:D].rearrange("p (h c) -> p h c", h=H)
                    V.tensor_tensor(xv, xv, bc(ex[:, k * H:(k + 1) * H].unsqueeze(2), [BN, H, C]), ALU.mult)
                    V.tensor_tensor(x[:, D:D + H], x[:, D:D + H], ex[:, k * H:(k + 1) * H], ALU.mult)
                dve.drain()
                V.tensor_tensor(ST[:, 0:D + H], ST[:, 0:D + H], acc[:, 0:D + H], ALU.add)
                if gat:
                    V.scalar_tensor_tensor(out=ST[:, NC - 5:NC], in0=ST[:, NC - 5:NC], scalar=g["keep_t"][0:BN, sc],
                                           in1=acc[:, NC - 5:NC], op0=ALU.mult, op1=ALU.add)
                dve.drain()
                V.tensor_copy(RES[:, bass.ds(blk, 1), 0:NC].rearrange("p a f -> p (a f)"), ST[:])
            dve.drain()


def sum_pass(g, name, table):
    nc, a, RES = (g[k] for k in ("nc", "a", "RES"))
    with ExitStack() as ctx:
        sb = lambda n, s, dt=F32: ctx.enter_context(nc.sbuf_tensor(name + n, s, dt))
        sem = phase_semaphores(nc, ctx, name)
        G = sb("G", [128, T, D])
        src = sb("src", [128, T], I32)
        dst3 = sb("dst3", [128, T + 2], I32)
        dstf = sb("dstf", [128, T + 2])
        O = sb("O", [128, T, BN])
        ST = sb("ST", [BN, D])
        psA = ctx.enter_context(nc.psum_tensor(name + "psA", [128, 512], F32))
        S = {n: sem(n) for n in ("waited", "edges_in", "edges_used", "slots_free", "targets_ready", "sums_done", "sums_free")}
        gathered = [sem(f"gathered{b}") for b in range(NG)]
        block = ctx.enter_context(nc.Block())

        @block.sync
        def _(sp):
            load_steps(nc, sp, g, a, [(src, "src_p"), (dst3, "dst_p")], S["edges_in"],
                       (None, [(gathered[-1], 16 * len(BATCH[-1])), (S["edges_used"], 1)]))

        @block.gpsimd
        def _(pool):
            with pool.Fori(0, g["n_steps"](pool)) as s:
                pool.wait_ge(S["edges_in"], s * 32 + 32)
                for b, tiles in enumerate(BATCH):
                    pool.wait_ge(S["slots_free"], s * NG + b + 1)
                    pool.sem_inc(S["waited"], 1)
                    for t in tiles:
                        nc.gpsimd.indirect_dma_start(
                            out=G[:, t, :], out_offset=None, in_=table,
                            in_offset=bass.IndirectOffsetOnAxis(ap=src[:, t:t + 1], axis=0)).then_inc(gathered[b], 16)

        @block.tensor
        def _(pe):
            pe.sem_inc(S["slots_free"], NG)
            with pe.Fori(0, g["n_steps"](pe)) as s:
                pe.wait_ge(S["targets_ready"], s + 1)
                pe.wait_ge(S["sums_free"], s + 1)
                for b, tiles in enumerate(BATCH):
                    pe.wait_ge(gathered[b], s * (16 * len(tiles)) + 16 * len(tiles))
                    for t in tiles:
                        mmi = nc.tensor.matmul(psA[0:BN, 0:D], O[:, t, :], G[:, t, :], start=(t == 0), stop=(t == T - 1))
                    if b < NG - 1:
                        mmi.then_inc(S["slots_free"], 1)
                mmi.then_inc(S["sums_done"], 1)
                pe.wait_ge(S["sums_done"], s + 1)
                pe.sem_inc(S["slots_free"], 1)

        @block.vector
        def _(dve):
            V = nc.vector
            V.memset(ST[:], 0.0)
            dve.drain()
            dve.sem_inc(S["sums_free"], 1)
            with dve.Fori(0, g["n_steps"](dve)) as s:
                blk = dve.value_load(g["steps_i"][0:1, bass.ds(s, 1)], min_val=0, max_val=NB - 1)
                sc = bass.ds(s, 1)
                dve.wait_ge(S["edges_in"], s * 32 + 32)
                V.tensor_scalar(dstf[:], dst3[:], g["base_t"][:, sc], None, ALU.subtract).then_inc(S["edges_used"], 1)
                dve.drain()
                V.tensor_tensor(O[:], g["iota"][:, 0:BN].unsqueeze(1).broadcast_to([128, T, BN]),
                                dstf[:, 1:T + 1].unsqueeze(2).broadcast_to([128, T, BN]), ALU.is_equal).then_inc(S["targets_ready"], 1)
                dve.wait_ge(S["sums_done"], s + 1)
                V.scalar_tensor_tensor(out=ST[:], in0=ST[:], scalar=g["keep_t"][0:BN, sc], in1=psA[0:BN, 0:D],
                                       op0=ALU.mult, op1=ALU.add).then_inc(S["sums_free"], 1)
                dve.drain()
                V.tensor_copy(RES[:, bass.ds(blk, 1), 0:D].rearrange("p a f -> p (a f)"), ST[:])
            dve.drain()


def relation_pass(g, name, table):
    nc, a, RES, X = (g[k] for k in ("nc", "a", "RES", "X"))
    NBAS = 8
    HB = NBAS // 2
    with ExitStack() as ctx:
        sb = lambda n, s, dt=F32: ctx.enter_context(nc.sbuf_tensor(name + n, s, dt))
        sem = phase_semaphores(nc, ctx, name)
        G = sb("G", [128, T, D])
        src = sb("src", [128, T], I32)
        dst3 = sb("dst3", [128, T + 2], I32)
        wgt = sb("wgt", [128, T])
        typ = sb("typ", [64, CH], I32)
        tyo = sb("tyo", [64, CH])
        wc = sb("wc", [64, NBAS])
        coef = sb("coef", [128, T, NBAS])
        dstf = sb("dstf", [128, T + 2])
        O = sb("O", [128, T, BN])
        CO = sb("CO", [128, 4, NBAS, BN])
        ST = sb("ST", [D, NBAS, BN])
        bases = sb("bases", [D, NBAS, D])
        loopw = sb("loopw", [D, D])
        XB = sb("XB", [BN, D])
        xT = sb("xT", [D, BN])
        psA = ctx.enter_context(nc.psum_tensor(name + "psA", [128, 2, 512], F32))
        psC = ctx.enter_context(nc.psum_tensor(name + "psC", [128, 512], F32))
        psX = ctx.enter_context(nc.psum_tensor(name + "psX", [128, 512], F32))
        psR = ctx.enter_context(nc.psum_tensor(name + "psR", [128, 512], F32))
        S = {n: sem(n) for n in ("consts", "waited", "edges_in", "edges_used", "slots_free", "types_ready", "coef_made", "coef_used", "products_ready",
                                 "products_used", "sums_done", "sums_free", "block_ready", "block_turned", "block_copied", "rows_done",
                                 "rows_used")}
        gathered = [sem(f"gathered{b}") for b in range(NG)]
        block = ctx.enter_context(nc.Block())

        @block.sync
        def _(sp):
            sp.dma_start(wc[:], a["L1_gnn_w_comp"]).then_inc(S["consts"], 16)
            sp.dma_start(bases[:], a["L1_gnn_weight"].rearrange("b i o -> i b o")).then_inc(S["consts"], 16)
            sp.dma_start(loopw[:], a["L1_gnn_loop_weight"]).then_inc(S["consts"], 16)
            load_steps(nc, sp, g, a, [(src, "src_p"), (dst3, "dst_p"), (typ, "type_p"), (wgt, "weight_p")], S["edges_in"],
                       (None, [(gathered[-1], 16 * len(BATCH[-1])), (S["edges_used"], 1)]))

        @block.gpsimd
        def _(pool):
            with pool.Fori(0, g["n_steps"](pool)) as s:
                pool.wait_ge(S["edges_in"], s * 64 + 64)
                for b, tiles in enumerate(BATCH):
                    pool.wait_ge(S["slots_free"], s * NG + b + 1)
                    pool.sem_inc(S["waited"], 1)
                    pool.sem_inc(S["waited"], 1)
                    for t in tiles:
                        nc.gpsimd.indirect_dma_start(
                            out=G[:, t, :], out_offset=None, in_=table,
                            in_offset=bass.IndirectOffsetOnAxis(ap=src[:, t:t + 1], axis=0)).then_inc(gathered[b], 16)

        @block.tensor
        def _(pe):
            pe.sem_inc(S["slots_free"], NG)
            pe.wait_ge(S["consts"], 48)
            with pe.Fori(0, g["n_steps"](pe)) as s:
                pe.wait_ge(S["types_ready"], s + 1)
                onehot = tyo[:].rearrange("r (p t) -> r t p", t=T)
                for t in range(T):
                    mmi = nc.tensor.matmul(psC[:, t * NBAS:(t + 1) * NBAS], onehot[:, t, :], wc[:], start=True, stop=True)
                mmi.then_inc(S["coef_made"], 1)
                pe.wait_ge(S["block_ready"], s + 1)
                nc.tensor.transpose(psX[:, 0:BN], XB[:], g["eye"][0:BN, 0:BN]).then_inc(S["block_turned"], 1)
                pe.wait_ge(S["sums_free"], s + 1)
                for b, tiles in enumerate(BATCH):
                    pe.wait_ge(gathered[b], s * (16 * len(tiles)) + 16 * len(tiles))
                    for t in tiles:
                        pe.wait_ge(S["products_ready"], s * T + t + 1)
                        for k in range(2):
                            mmi = nc.tensor.matmul(psA[:, k, 0:HB * BN], G[:, t, :],
                                                   CO[:, t % 4, k * HB:(k + 1) * HB, :].rearrange("p b d -> p (b d)"),
                                                   start=(t == 0), stop=(t == T - 1))
                        mmi.then_inc(S["products_used"], 1)
                    pe.wait_ge(S["products_used"], s * T + tiles[-1] + 1)
                    pe.sem_inc(S["slots_free"], 1)
                mmi = nc.tensor.matmul(psR[0:1, 0:1], wc[0:1, 0:1], wc[0:1, 0:1], start=True, stop=True)
                mmi.then_inc(S["sums_done"], 1)
                pe.wait_ge(S["block_copied"], s + 1)
                pe.wait_ge(S["rows_used"], s * 2 + 2)
                for k in range(NBAS):
                    nc.tensor.matmul(psR[0:BN, 0:D], ST[:, k, :], bases[:, k, :], start=(k == 0), stop=False)
                nc.tensor.matmul(psR[0:BN, 0:D], xT[:], loopw[:], start=False, stop=True).then_inc(S["rows_done"], 1)

        @block.vector
        def _(dve):
            V = nc.vector
            V.memset(ST[:], 0.0)
            dve.drain()
            dve.sem_inc(S["sums_free"], 1)
            dve.sem_inc(S["rows_used"], 1)
            with dve.Fori(0, g["n_steps"](dve)) as s:
                blk = dve.value_load(g["steps_i"][0:1, bass.ds(s, 1)], min_val=0, max_val=NB - 1)
                sc = bass.ds(s, 1)
                dve.wait_ge(S["edges_in"], s * 64 + 64)
                V.tensor_scalar(tyo[:], typ[:], g["iota_p"][0:64, 0:1], None, ALU.is_equal).then_inc(S["types_ready"], 1)
                V.tensor_copy(XB[:], X[:, bass.ds(blk, 1), :].rearrange("p a f -> p (a f)")).then_inc(S["block_ready"], 1)
                V.tensor_scalar(dstf[:], dst3[:], g["base_t"][:, sc], None, ALU.subtract)
                dve.drain()
                V.tensor_tensor(O[:], g["iota"][:, 0:BN].unsqueeze(1).broadcast_to([128, T, BN]),
                                dstf[:, 1:T + 1].unsqueeze(2).broadcast_to([128, T, BN]), ALU.is_equal)
                dve.wait_ge(S["coef_made"], s + 1)
                V.tensor_tensor(coef[:], psC[:, 0:T * NBAS].rearrange("p (t b) -> p t b", b=NBAS),
                                wgt[:].unsqueeze(2).broadcast_to([128, T, NBAS]), ALU.mult).then_inc(S["edges_used"], 1)
                dve.drain()
                for t in range(T):
                    if t >= 4:
                        dve.wait_ge(S["products_used"], s * T + t - 3)
                    V.tensor_tensor(CO[:, t % 4], O[:, t:t + 1, :].broadcast_to([128, NBAS, BN]),
                                    coef[:, t, :].unsqueeze(2).broadcast_to([128, NBAS, BN]), ALU.mult).then_inc(S["products_ready"], 1)
                    if t == 1:
                        dve.wait_ge(S["block_turned"], s + 1)
                        V.tensor_copy(xT[:], psX[:, 0:BN]).then_inc(S["block_copied"], 1)
                dve.wait_ge(S["sums_done"], s + 1)
                V.scalar_tensor_tensor(out=ST[:, 0:HB, :], in0=ST[:, 0:HB, :], scalar=g["keep_t"][:, sc],
                                       in1=psA[:, 0, 0:HB * BN].rearrange("p (b d) -> p b d", d=BN), op0=ALU.mult, op1=ALU.add)
                V.scalar_tensor_tensor(out=ST[:, HB:, :], in0=ST[:, HB:, :], scalar=g["keep_t"][:, sc],
                                       in1=psA[:, 1, 0:HB * BN].rearrange("p (b d) -> p b d", d=BN), op0=ALU.mult, op1=ALU.add)
                dve.drain()
                dve.sem_inc(S["sums_free"], 1)
                dve.sem_inc(S["rows_used"], 1)
                dve.wait_ge(S["rows_done"], s + 1)
                V.tensor_copy(RES[:, bass.ds(blk, 1), 0:D].rearrange("p a f -> p (a f)"), psR[0:BN, 0:D]).then_inc(S["rows_used"], 1)
                dve.drain()


def finish_parts(g, name, work, loads=(), n_sqrt=0, store=None, exps=None):
    nc, a = g["nc"], g["a"]
    with ExitStack() as ctx:
        sb = lambda n, s, dt=F32: ctx.enter_context(nc.sbuf_tensor(name + n, s, dt))
        sem = phase_semaphores(nc, ctx, name)
        mean = sb("mean", [BN, NB])
        var = sb("var", [BN, NB])
        tmp = sb("tmp", [BN, NB, D])
        row = {n: sb(n, [BN, D]) for n in loads}
        sm = sb("sm", [BN, NB, 32])
        loaded, asked, rooted, stored = (sem(n) for n in ("loaded", "asked", "rooted", "stored"))
        block = ctx.enter_context(nc.Block())

        @block.sync
        def _(sp):
            for n in loads:
                sp.dma_start(row[n][:], a[n].partition_broadcast(BN)).then_inc(loaded, 16)
            if store is not None:
                sp.wait_ge(asked, n_sqrt + 1)
                src, dst = store
                sp.dma_start(dst.rearrange("(b p) f -> p b f", p=BN)[:], src[:, 0:NB, :]).then_inc(stored, 16) if N == NP else None
                full = N // BN
                sp.dma_start(dst[0:full * BN].rearrange("(b p) f -> p b f", p=BN), src[:, 0:full, :]).then_inc(stored, 16)
                sp.dma_start(dst[full * BN:N], src[0:N - full * BN, full, :]).then_inc(stored, 16)
                sp.wait_ge(stored, 32)

        @block.scalar
        def _(act):
            k = 0
            if exps:
                act.wait_ge(asked, 1)
                nc.scalar.activation(sm[:, :, 0:exps], sm[:, :, 0:exps], ACT.Exp).then_inc(rooted, 1)
                k = 1
            for i in range(n_sqrt):
                act.wait_ge(asked, k + i + 1)
                nc.scalar.activation(var[:], var[:], ACT.Sqrt).then_inc(rooted, 1)

        @block.vector
        def _(dve):
            dve.wait_ge(loaded, 16 * len(loads)) if loads else None
            work(dve, nc.vector, row, mean, var, tmp, sm, asked, rooted)
            dve.drain()
            nc.vector.memset(sm[:, :, 31:32], 0.0).then_inc(asked, 1)


def rows_of(x):
    return x[:].unsqueeze(1).broadcast_to([BN, NB, D])


def gat_finish(g):
    nc, X, RES, Q, SKIP, cnt1 = (g[k] for k in ("nc", "X", "RES", "Q", "SKIP", "cnt1"))
    H, C = 4, 32

    def work(dve, V, row, mean, var, tmp, sm, asked, rooted):
        dr = dve.drain
        b4 = lambda x: x.broadcast_to([BN, NB, H])
        plain = D + 2 * H + 1
        V.tensor_copy(cnt1[:], RES[:, :, plain + 4])
        dr()
        V.tensor_scalar(mean[:], cnt1[:], 1.0, None, ALU.max)
        dr()
        V.reciprocal(mean[:], mean[:])
        dr()
        al = sm[:, :, 8:12]
        V.tensor_tensor(al, RES[:, :, plain:plain + 4], b4(mean[:].unsqueeze(2)), ALU.mult)
        dr()
        V.tensor_tensor(al, al, Q[:, :, 0:4], ALU.add)
        dr()
        V.tensor_tensor(al, al, Q[:, :, 4:8], ALU.add)
        dr()
        V.scalar_tensor_tensor(out=al, in0=al, scalar=0.2, in1=al, op0=ALU.mult, op1=ALU.max)
        dr()
        m = sm[:, :, 12:16]
        V.tensor_tensor(m, RES[:, :, D + H:D + 2 * H], al, ALU.max)
        dr()
        V.tensor_tensor(sm[:, :, 0:4], RES[:, :, D + H:D + 2 * H], m, ALU.subtract)
        V.tensor_tensor(sm[:, :, 4:8], al, m, ALU.subtract)
        dr()
        V.memset(sm[:, :, 30:31], 0.0).then_inc(asked, 1)
        dve.wait_ge(rooted, 1)
        den = sm[:, :, 12:16]
        V.tensor_tensor(den, RES[:, :, D:D + H], sm[:, :, 0:4], ALU.mult)
        dr()
        V.tensor_tensor(den, den, sm[:, :, 4:8], ALU.add)
        dr()
        V.tensor_scalar(den, den, 1e-16, None, ALU.add)
        dr()
        V.reciprocal(den, den)
        dr()
        V.tensor_tensor(sm[:, :, 0:4], sm[:, :, 0:4], den, ALU.mult)
        V.tensor_tensor(sm[:, :, 4:8], sm[:, :, 4:8], den, ALU.mult)
        dr()
        for h in range(H):
            hs = slice(h * C, (h + 1) * C)
            V.tensor_tensor(tmp[:, :, hs], RES[:, :, hs], sm[:, :, h:h + 1].broadcast_to([BN, NB, C]), ALU.mult)
            V.tensor_tensor(SKIP[:, :, hs], SKIP[:, :, hs], sm[:, :, 4 + h:5 + h].broadcast_to([BN, NB, C]), ALU.mult)
        dr()
        y = RES[:, :, 0:D]
        V.tensor_tensor(y, tmp[:], SKIP[:], ALU.add)
        dr()
        V.tensor_tensor(y, y, rows_of(row["L0_gnn_bias"]), ALU.add)
        dr()
        V.tensor_tensor(y, y, X[:], ALU.add)
        dr()
        layernorm(nc, dve, rooted, asked, y, mean, var, tmp, 2)
        V.tensor_tensor(y, y, rows_of(row["L0_gnn_ln_gamma"]), ALU.mult)
        dr()
        V.tensor_tensor(y, y, rows_of(row["L0_gnn_ln_beta"]), ALU.add)
        dr()
        V.scalar_tensor_tensor(out=X[:], in0=y, scalar=0.0, in1=X[:], op0=ALU.max, op1=ALU.add)
        dr()
        layernorm(nc, dve, rooted, asked, X, mean, var, tmp, 3)
        V.tensor_scalar(var[:], cnt1[:], 1.0, None, ALU.add).then_inc(asked, 1)
        dve.wait_ge(rooted, 4)
        V.reciprocal(cnt1[:], var[:])

    finish_parts(g, "f0", work, ("L0_gnn_bias", "L0_gnn_ln_gamma", "L0_gnn_ln_beta"), n_sqrt=3, exps=8)


def relation_finish(g):
    nc, X, RES = (g[k] for k in ("nc", "X", "RES"))

    def work(dve, V, row, mean, var, tmp, sm, asked, rooted):
        y = RES[:, :, 0:D]
        V.tensor_tensor(y, y, rows_of(row["L1_gnn_h_bias"]), ALU.add)
        dve.drain()
        V.scalar_tensor_tensor(out=X[:], in0=y, scalar=0.0, in1=X[:], op0=ALU.max, op1=ALU.add)
        dve.drain()
        layernorm(nc, dve, rooted, asked, X, mean, var, tmp, 1)

    finish_parts(g, "f1", work, ("L1_gnn_h_bias",), n_sqrt=1)


def transformer_finish(g, name, H, last):
    nc, X, RES, SKIP = (g[k] for k in ("nc", "X", "RES", "SKIP"))
    C = D // H

    def work(dve, V, row, mean, var, tmp, sm, asked, rooted):
        den = sm[:, :, 0:H]
        V.tensor_scalar(den, RES[:, :, D:D + H], 1e-16, None, ALU.add)
        dve.drain()
        V.reciprocal(den, den)
        dve.drain()
        y = RES[:, :, 0:D]
        for h in range(H):
            V.tensor_tensor(RES[:, :, h * C:(h + 1) * C], RES[:, :, h * C:(h + 1) * C],
                            sm[:, :, h:h + 1].broadcast_to([BN, NB, C]), ALU.mult)
        dve.drain()
        V.tensor_tensor(y, y, SKIP[:], ALU.add)
        dve.drain()
        if last:
            V.tensor_tensor(X[:], X[:], y, ALU.add)
            dve.drain()
            layernorm(nc, dve, rooted, asked, X, mean, var, tmp, 1)

    finish_parts(g, name, work, (), n_sqrt=1 if last else 0)


def gcn_finish(g, name, bias, out):
    nc, X, RES, SKIP, cnt1 = (g[k] for k in ("nc", "X", "RES", "SKIP", "cnt1"))

    def work(dve, V, row, mean, var, tmp, sm, asked, rooted):
        y = RES[:, :, 0:D]
        V.tensor_tensor(y, y, SKIP[:], ALU.add)
        dve.drain()
        V.tensor_tensor(y, y, cnt1[:].unsqueeze(2).broadcast_to([BN, NB, D]), ALU.mult)
        dve.drain()
        V.tensor_tensor(y, y, rows_of(row[bias]), ALU.add)
        dve.drain()
        if out is None:
            V.tensor_scalar(y, y, 0.0, None, ALU.max)
        else:
            V.tensor_tensor(X[:], X[:], y, ALU.add)
            dve.drain()
            layernorm(nc, dve, rooted, asked, X, mean, var, tmp, 1)

    finish_parts(g, name, work, (bias,), n_sqrt=0 if out is None else 1, store=None if out is None else (X, out))


def kernel(**inputs):
    import numpy as np
    import concourse.bacc as bacc
    from concourse import mybir as mb
    from concourse.bass_utils import run_bass_kernel_spmd

    def padded(v, front, back, fill):
        v = np.asarray(v)
        out = np.full((front + v.shape[0] + back,) + v.shape[1:], fill, v.dtype)
        out[front:front + v.shape[0]] = v
        return out

    FAR = 1 << 20
    E_ROWS = 128 * (E // 128 + 1)
    arrays = {
        "x": padded(inputs["x"], 0, NP - N, 0),
        "src_p": padded(inputs["src"], 0, CH, 0),
        "dst_p": padded(inputs["dst"], 1, CH + 1, FAR),
        "dst_rows": padded(inputs["dst"], 0, E_ROWS - E, FAR).reshape(128, E_ROWS // 128),
        "attr_p": padded(inputs["edge_attr_13"], 0, CH, 0),
        "type_p": padded(inputs["edge_type_64"], 0, CH, 0),
        "weight_p": padded(np.asarray(inputs["edge_weight1"]).reshape(E), 0, CH, 0),
        "eye": np.eye(128, dtype=np.float32),
        "iota": np.arange(128, dtype=np.float32),
        "more": np.arange(1, MORE + 1, dtype=np.float32) * np.float32(CH),
    }
    for k, v in inputs.items():
        if k[0] == "L":
            arrays[k] = np.ascontiguousarray(v)
    nc = bacc.Bacc("TRN2", target_bir_lowering=False, num_devices=1)
    arrays = {f"in_{k}": v for k, v in arrays.items()}
    aps = {k[3:]: nc.dram_tensor(k, v.shape, mb.dt.from_np(v.dtype), kind="ExternalInput").ap() for k, v in arrays.items()}
    out = nc.dram_tensor("out", (N, D), F32, kind="ExternalOutput").ap()
    build(nc, aps, out)
    r = run_bass_kernel_spmd(nc, [arrays], core_ids=[0])
    return r.results[0]["out"]
```

```python
from contextlib import ExitStack

import concourse.bass as bass
from concourse import mybir

ALU = mybir.AluOpType
ACT = mybir.ActivationFunctionType
AX = mybir.AxisListType
F32 = mybir.dt.float32
I32 = mybir.dt.int32
F16 = mybir.dt.float16

N = 3125
E = 103125
D = 128
BN = 121
NB = 26
NP = NB * BN
T = 33
CH = 128 * T
MORE = E // CH
SMAX = NB + MORE
BIG = 1.0e30
BATCH = [list(range(g, min(g + 4, T))) for g in range(0, T, 4)]
NG = len(BATCH)
EPS = 1e-5
SLOTS = 64
PAIRS = (BN + 1) // 2
CB = 9
BANKS = -(-PAIRS // CB)
HI = 4
HBANKS = -(-NB // HI)
NT = -(-E // 128)
GT = 13
TB = [list(range(0, 5)), list(range(5, 9)), list(range(9, 13))]
TBMAX = max(len(b) for b in TB)
WIN = 32
ROUND = 1.5 * 2 ** 23


def phase_semaphores(nc, ctx, name):
    own = []

    def clear():
        nc.clear_and_free_semaphores(own)
        nc.all_engine_barrier()

    ctx.callback(clear)

    def sem(n):
        own.append(nc.alloc_semaphore(name=name + n))
        return own[-1]

    return sem


def layernorm(nc, dve, act_sem, dve_sem, y, mean, var, tmp, count):
    inv = 1.0 / D
    nc.vector.tensor_reduce(mean[:], y[:], AX.X, ALU.add)
    dve.drain()
    nc.vector.tensor_scalar(mean[:], mean[:], inv, None, ALU.mult)
    dve.drain()
    nc.vector.tensor_tensor(y[:], y[:], mean[:].unsqueeze(2).broadcast_to([BN, NB, D]), ALU.subtract)
    dve.drain()
    nc.vector.tensor_tensor(tmp[:], y[:], y[:], ALU.mult)
    dve.drain()
    nc.vector.tensor_reduce(var[:], tmp[:], AX.X, ALU.add)
    dve.drain()
    nc.vector.tensor_scalar(var[:], var[:], inv, EPS, ALU.mult, ALU.add).then_inc(dve_sem, 1)
    dve.wait_ge(act_sem, count)
    nc.vector.reciprocal(var[:], var[:])
    dve.drain()
    nc.vector.tensor_tensor(y[:], y[:], var[:].unsqueeze(2).broadcast_to([BN, NB, D]), ALU.mult)
    dve.drain()


def build(nc, a, out):
    with ExitStack() as top:
        def keep(name, shape, dt=F32):
            return top.enter_context(nc.sbuf_tensor(name, shape, dt))

        X = keep("X", [BN, NB, D])
        RES = keep("RES", [BN, NB, 152])
        Q = keep("Q", [BN, NB, D])
        SKIP = keep("SKIP", [BN, NB, D])
        eye = keep("eye", [128, 128])
        iota = keep("iota", [128, 128])
        pidx = keep("pidx", [128, 1])
        base_t = keep("base_t", [128, SMAX])
        basep_t = keep("basep_t", [128, SMAX])
        neg_t = keep("neg_t", [128, SMAX])
        keep_t = keep("keep_t", [128, SMAX])
        steps_i = keep("steps_i", [1, 2 * SMAX + 2], I32)
        cnt1 = keep("cnt1", [BN, NB])
        deg = keep("deg", [BN, NB])
        more_i = keep("more_i", [1, 1], I32)
        wide_i = keep("wide_i", [1, 1], I32)
        counts = nc.dram_tensor("counts", [NB, BN, NP], F32).ap()

        tab = {w: nc.dram_tensor(f"table_{w}", [NP, w], F32).ap() for w in (132, 128, 256)}

        def n_steps(eng):
            return eng.value_load(steps_i[0:1, 2 * SMAX:2 * SMAX + 1], min_val=NB, max_val=SMAX)

        def is_wide(eng):
            return eng.value_load(wide_i[:], min_val=0, max_val=1)

        plan_steps(nc, a, X, eye, iota, pidx, base_t, basep_t, neg_t, keep_t, steps_i)
        g = dict(iota_p=pidx, nc=nc, a=a, X=X, RES=RES, Q=Q, SKIP=SKIP, eye=eye, iota=iota, base_t=base_t,
                 basep_t=basep_t, neg_t=neg_t, keep_t=keep_t, steps_i=steps_i, n_steps=n_steps, cnt1=cnt1,
                 deg=deg, more_i=more_i, counts=counts, wide_i=wide_i,
                 is_wide=is_wide)

        project(g, "p0", [("L0_gnn_W", None, 0.0)], tab[132], "gat")
        attention_pass(g, "e0", tab[132], 132, 4, True)
        gat_finish(g)
        count_neighbours(g)
        count_neighbours_any(g)
        project(g, "p1", [], tab[128], "copy")
        tile_tables(g)
        relation_tiles(g, "t1", tab[128])
        relation_pass(g, "e1", tab[128])
        relation_finish(g)
        for c, heads in ((1, 8), (2, 1)):
            ws = [(f"L2_gnn_W{n}{c}", f"L2_gnn_b{n}{c}", 0.0) for n in "kvqs"]
            if c == 2:
                src = RES
            project(g, f"p2{c}", ws, tab[256], "qkv", scale=float(D // heads) ** -0.5, source=X if c == 1 else RES)
            attention_pass(g, f"e2{c}", tab[256], 256, heads, False)
            transformer_finish(g, f"f2{c}", heads, last=(c == 2))
        for c in (1, 2):
            project(g, f"p3{c}", [(f"L3_gnn_W{c}", None, 0.0)], tab[128], "gcn", source=X if c == 1 else RES)
            dense_sum(g, f"e3{c}")
            gcn_finish(g, f"f3{c}", f"L3_gnn_b{c}", out if c == 2 else None)


def plan_steps(nc, a, X, eye, iota, pidx, base_t, basep_t, neg_t, keep_t, steps_i):
    PF = E // 128 + 1
    with ExitStack() as ctx:
        sb = lambda n, s, dt=F32: ctx.enter_context(nc.sbuf_tensor(n, s, dt))
        sem = phase_semaphores(nc, ctx, "plan")
        dsti = sb("dsti", [128, PF], I32)
        below = sb("below", [128, PF])
        part = sb("part", [128, NB + 1])
        ones = sb("ones", [128, 128])
        cum = sb("cum", [1, NB + 1])
        cnt = sb("cnt", [1, NB])
        nst = sb("nst", [1, NB])
        endn = sb("endn", [1, NB])
        zero = sb("zero", [1, NB])
        big1 = sb("big1", [1, NB, MORE])
        past = sb("past", [1, SMAX, NB])
        prod = sb("prod", [1, SMAX, NB])
        row = sb("row", [1, 6, SMAX])
        ch = sb("ch", [1, MORE])
        ps = ctx.enter_context(nc.psum_tensor("ps_plan", [128, 512], F32))
        ps2 = ctx.enter_context(nc.psum_tensor("ps_plan2", [128, 512], F32))
        loaded, counted, summed, ready, spread = (sem(n) for n in ("loaded", "counted", "summed", "ready", "spread"))
        block = ctx.enter_context(nc.Block())

        @block.sync
        def _(sp):
            sp.dma_start(dsti[:], a["dst_rows"]).then_inc(loaded, 16)
            sp.dma_start(X[:], a["x"].rearrange("(b p) f -> p b f", p=BN)).then_inc(loaded, 16)
            sp.dma_start(eye[:], a["eye"]).then_inc(loaded, 16)
            sp.dma_start(iota[:], a["iota"].partition_broadcast(128)).then_inc(loaded, 16)
            sp.dma_start(pidx[:], a["iota"].rearrange("(p a) -> p a", a=1)).then_inc(loaded, 16)
            sp.dma_start(ch[:], a["more"].rearrange("(a p) -> a p", a=1)).then_inc(loaded, 16)

        @block.vector
        def _(dve):
            dve.wait_ge(loaded, 96)
            nc.vector.memset(ones[:], 1.0)
            nc.vector.memset(zero[:], 0.0)
            for b in range(NB + 1):
                nc.vector.tensor_scalar(below[:], dsti[:], float(b * BN) if b < NB else float(NP), None, ALU.is_lt)
                dve.drain()
                nc.vector.tensor_reduce(part[:, b:b + 1], below[:], AX.X, ALU.add)
                dve.drain()
            nc.vector.memset(row[:], 0.0).then_inc(counted, 1)
            dve.wait_ge(summed, 1)
            nc.vector.tensor_copy(cum[:], ps[0:1, 0:NB + 1])
            dve.drain()
            nc.vector.tensor_tensor(cnt[:], cum[:, 1:NB + 1], cum[:, 0:NB], ALU.subtract)
            dve.drain()
            nc.vector.tensor_tensor(big1[:], cnt[:].unsqueeze(2).broadcast_to([1, NB, MORE]),
                                    ch[:].unsqueeze(1).broadcast_to([1, NB, MORE]), ALU.is_gt)
            dve.drain()
            nc.vector.tensor_reduce(nst[:], big1[:], AX.X, ALU.add)
            dve.drain()
            nc.vector.tensor_scalar(nst[:], nst[:], 1.0, None, ALU.add)
            dve.drain()
            nc.vector.tensor_tensor_scan(endn[:], nst[:], zero[:], 0.0, ALU.add, ALU.add)
            dve.drain()
            nc.vector.tensor_tensor(past[:], endn[:].unsqueeze(1).broadcast_to([1, SMAX, NB]),
                                    iota[0:1, 0:SMAX].unsqueeze(2).broadcast_to([1, SMAX, NB]), ALU.is_le)
            dve.drain()
            nc.vector.tensor_reduce(row[:, 0, :], past[:], AX.X, ALU.add)
            for k, v in ((1, cnt), (2, nst)):
                nc.vector.tensor_tensor(prod[:], past[:], v[:].unsqueeze(1).broadcast_to([1, SMAX, NB]), ALU.mult)
                dve.drain()
                nc.vector.tensor_reduce(row[:, k, :], prod[:], AX.X, ALU.add)
                dve.drain()
            nc.vector.tensor_tensor(row[:, 2, :], iota[0:1, 0:SMAX], row[:, 2, :], ALU.subtract)
            dve.drain()
            nc.vector.scalar_tensor_tensor(out=row[:, 1, :], in0=row[:, 2, :], scalar=float(CH), in1=row[:, 1, :],
                                           op0=ALU.mult, op1=ALU.add)
            nc.vector.tensor_scalar(row[:, 3, :], row[:, 2, :], 0.0, None, ALU.is_equal)
            dve.drain()
            nc.vector.tensor_scalar(row[:, 4, :], row[:, 3, :], -BIG, None, ALU.mult)
            nc.vector.tensor_scalar(row[:, 5, :], row[:, 3, :], -1.0, 1.0, ALU.mult, ALU.add)
            dve.drain()
            nc.vector.tensor_scalar(row[:, 3, :], row[:, 0, :], float(BN), None, ALU.mult)
            nc.vector.tensor_scalar(row[:, 0, :], row[:, 0, :], float(NB - 1), None, ALU.min)
            nc.vector.tensor_scalar(row[:, 1, :], row[:, 1, :], float(E), None, ALU.min)
            dve.drain()
            nc.vector.tensor_copy(steps_i[:, 0:SMAX], row[:, 0, :])
            nc.vector.tensor_copy(steps_i[:, SMAX:2 * SMAX], row[:, 1, :])
            nc.vector.tensor_copy(steps_i[:, 2 * SMAX:2 * SMAX + 1], endn[:, NB - 1:NB])
            dve.drain()
            nc.vector.memset(zero[:], 0.0).then_inc(ready, 1)
            dve.wait_ge(spread, 1)
            nc.vector.tensor_copy(base_t[:], ps2[:, 0:SMAX])
            nc.vector.tensor_scalar(basep_t[:], ps2[:, 0:SMAX], pidx[:, 0:1], None, ALU.add)
            nc.vector.tensor_copy(neg_t[:], ps2[:, SMAX:2 * SMAX])
            nc.vector.tensor_copy(keep_t[:], ps2[:, 2 * SMAX:3 * SMAX])
            dve.drain()

        @block.tensor
        def _(pe):
            pe.wait_ge(counted, 1)
            nc.tensor.matmul(ps[0:1, 0:NB + 1], ones[:, 0:1], part[:], start=True, stop=True).then_inc(summed, 1)
            pe.wait_ge(ready, 1)
            nc.tensor.matmul(ps2[:, 0:3 * SMAX], ones[0:1, :], row[:, 3:6, :], start=True, stop=True).then_inc(spread, 1)


def project(g, name, weights, table, kind, scale=1.0, source=None):
    nc, a, X, RES, Q, SKIP, eye, cnt1 = (g[k] for k in ("nc", "a", "X", "RES", "Q", "SKIP", "eye", "cnt1"))
    source = source or X
    W = D * len(weights)
    width = table.shape[1]
    with ExitStack() as ctx:
        sb = lambda n, s, dt=F32: ctx.enter_context(nc.sbuf_tensor(name + n, s, dt))
        sem = phase_semaphores(nc, ctx, name)
        if kind == "copy":
            stored = sem("stored")
            block = ctx.enter_context(nc.Block())

            @block.sync
            def _(sp):
                sp.dma_start(table.rearrange("(b p) f -> p b f", p=BN), source[:, :, 0:D]).then_inc(stored, 16)
                sp.wait_ge(stored, 16)
            return
        w = sb("w", [D, W])
        bias = sb("bias", [BN, W])
        xT = sb("xT", [D, 2, BN])
        rows = sb("rows", [BN, NB, width])
        att = sb("att", [BN, 2, D])
        tmp = sb("tmp", [BN, NB, D])
        psT = ctx.enter_context(nc.psum_tensor(name + "psT", [128, 2, 512], F32))
        psY = ctx.enter_context(nc.psum_tensor(name + "psY", [128, 2, 512], F32))
        loaded, turned, copied, made, used, stored, rooted = (
            sem(n) for n in ("loaded", "turned", "copied", "made", "used", "stored", "rooted"))
        n_loads = len(weights) + sum(b is not None for _, b, _ in weights) + 2 * (kind == "gat")
        block = ctx.enter_context(nc.Block())

        @block.sync
        def _(sp):
            for i, (wn, bn, _) in enumerate(weights):
                sp.dma_start(w[:, i * D:(i + 1) * D], a[wn]).then_inc(loaded, 16)
                if bn:
                    sp.dma_start(bias[:, i * D:(i + 1) * D], a[bn].partition_broadcast(BN)).then_inc(loaded, 16)
            if kind == "gat":
                for i, n in enumerate(("L0_gnn_att_src", "L0_gnn_att_dst")):
                    sp.dma_start(att[:, i, :], a[n].rearrange("h c -> (h c)").partition_broadcast(BN)).then_inc(loaded, 16)
            if kind == "gcn":
                return
            sp.wait_ge(used, NB + 1)
            sp.dma_start(table.rearrange("(b p) f -> p b f", p=BN), rows[:]).then_inc(stored, 16)
            sp.wait_ge(stored, 16)

        @block.tensor
        def _(pe):
            pe.wait_ge(loaded, 16 * n_loads)
            for b in range(NB + 1):
                if b < NB:
                    if b >= 2:
                        pe.wait_ge(copied, b - 1)
                    nc.tensor.transpose(psT[:, b % 2, 0:BN], source[:, b, 0:D], eye[0:BN, 0:BN]).then_inc(turned, 1)
                if b >= 1:
                    c = b - 1
                    pe.wait_ge(copied, c + 1)
                    if c >= 2:
                        pe.wait_ge(used, c - 1)
                    nc.tensor.matmul(psY[0:BN, c % 2, 0:W], xT[:, c % 2, :], w[:], start=True, stop=True).then_inc(made, 1)

        @block.scalar
        def _(act):
            for b in range(NB):
                act.wait_ge(turned, b + 1)
                if b >= 2:
                    act.wait_ge(made, b - 1)
                nc.scalar.copy(xT[:, b % 2, :], psT[:, b % 2, 0:BN]).then_inc(copied, 1)

        @block.vector
        def _(dve):
            dve.wait_ge(loaded, 16 * n_loads)
            for b in range(NB):
                dve.wait_ge(made, b + 1)
                if kind == "gat":
                    nc.vector.tensor_copy(rows[:, b, 4:4 + D], psY[0:BN, b % 2, 0:D]).then_inc(used, 1)
                elif kind == "gcn":
                    nc.vector.tensor_scalar(SKIP[:, b, :], psY[0:BN, b % 2, 0:D], cnt1[:, b:b + 1], None,
                                            ALU.mult).then_inc(used, 1)
                else:
                    nc.vector.tensor_tensor(rows[:, b, :], psY[0:BN, b % 2, 0:2 * D], bias[:, 0:2 * D], ALU.add)
                    nc.vector.tensor_tensor(Q[:, b, :], psY[0:BN, b % 2, 2 * D:3 * D], bias[:, 2 * D:3 * D], ALU.add)
                    nc.vector.tensor_tensor(SKIP[:, b, :], psY[0:BN, b % 2, 3 * D:4 * D], bias[:, 3 * D:4 * D],
                                            ALU.add).then_inc(used, 1)
            dve.drain()
            if kind == "gat":
                h = rows[:, :, 4:4 + D]
                for i in range(2):
                    nc.vector.tensor_tensor(tmp[:], h, att[:, i:i + 1, :].broadcast_to([BN, NB, D]), ALU.mult)
                    dve.drain()
                    dst = rows[:, :, 0:4] if i == 0 else Q[:, :, 0:4]
                    nc.vector.tensor_reduce(dst, tmp[:].rearrange("p b (h c) -> p b h c", h=4), AX.X, ALU.add)
                    dve.drain()
                nc.vector.tensor_copy(SKIP[:], h)
                nc.vector.tensor_copy(Q[:, :, 4:8], rows[:, :, 0:4])
            if kind == "qkv":
                nc.vector.tensor_scalar(Q[:], Q[:], scale, None, ALU.mult)
            dve.drain()
            nc.vector.memset(bias[:, 0:1], 0.0).then_inc(used, 1)


def load_steps(nc, sp, g, a, buffers, first, later):
    steps_i = g["steps_i"]
    done, sems = later

    def issue(s):
        e = sp.value_load(steps_i[0:1, bass.ds(s + SMAX, 1)], min_val=0, max_val=E)
        for buf, name in buffers:
            if name == "src_p":
                sp.dma_start(buf[:], a[name][bass.ds(e, CH)].rearrange("(p t) -> p t", p=128)).then_inc(first, 16)
            elif name == "dst_p":
                w = a[name][bass.ds(e, CH + 2)]
                w = bass.AP(w.tensor, w.offset, [[T, 128], [1, T + 2]])
                sp.dma_start(buf[:], w).then_inc(first, 16)
            elif name == "dst_all":
                sp.dma_start(buf[:], a["dst_p"][bass.ds(e + 1, CH)].partition_broadcast(BN)).then_inc(first, 16)
            elif name == "type_p":
                sp.dma_start(buf[:], a[name][bass.ds(e, CH)].partition_broadcast(64)).then_inc(first, 16)
            elif name == "weight_p":
                sp.dma_start(buf[:], a[name][bass.ds(e, CH)].rearrange("(p t) -> p t", p=128)).then_inc(first, 16)
            else:
                sp.dma_start(buf[:], a[name][bass.ds(e, CH), :].rearrange("(p t) c -> p (t c)", p=128)).then_inc(first, 16)

    issue(0)
    with sp.Fori(1, g["n_steps"](sp)) as s:
        for sem, each in sems:
            sp.wait_ge(sem, s * each)
        issue(s)


def attention_pass(g, name, table, width, H, gat):
    nc, a, RES, Q = (g[k] for k in ("nc", "a", "RES", "Q"))
    C = D // H
    vo = width - D
    wo, mo, fo = width, width + H, width + 2 * H
    extra = 5 if gat else 0
    GW = fo + 1 + extra
    NC = D + 2 * H + 1 + extra
    QW = 4 if gat else D
    with ExitStack() as ctx:
        sb = lambda n, s, dt=F32: ctx.enter_context(nc.sbuf_tensor(name + n, s, dt))
        sem = phase_semaphores(nc, ctx, name)
        G = sb("G", [128, T, GW])
        src = sb("src", [128, T], I32)
        dst3 = sb("dst3", [128, T + 2], I32)
        dstb = sb("dstb", [BN, CH], I32)
        dstf = sb("dstf", [128, T + 2])
        OT = sb("OT", [BN, CH])
        O = sb("O", [128, T, BN])
        ne = sb("ne", [128, T + 1])
        rb = sb("rb", [128, T + 1])
        hm = sb("hm", [128, T])
        tm = sb("tm", [128, T])
        Rf = sb("Rf", [128, H, T])
        Rb = sb("Rb", [128, H, T])
        A = sb("A", [128, H, T])
        Fw = sb("Fw", [128, H, T])
        M = sb("M", [128, H, T])
        X1 = sb("X1", [128, H, T])
        TI = sb("TI", [128, 6, H])
        TS = sb("TS", [H, 6, 128])
        UV = sb("UV", [H, 2, 128])
        LR = sb("LR", [H, 2, 128])
        ST = sb("ST", [BN, NC])
        acc = sb("acc", [BN, NC])
        mm = sb("mm", [BN, 3 * H])
        ex = sb("ex", [BN, 2 * H])
        if gat:
            attr = sb("attr", [128, T, 13], F32)
            wed = sb("wed", [128, 13, D])
            atte = sb("atte", [128, D])
            we = sb("we", [128, 4, 13])
            pr = sb("pr", [128, T, 13])
        psQ = ctx.enter_context(nc.psum_tensor(name + "psQ", [128, 3, 512], F32))
        psA = ctx.enter_context(nc.psum_tensor(name + "psA", [128, 512], F32))
        psT = ctx.enter_context(nc.psum_tensor(name + "psT", [128, 2, 512], F32))
        psB = ctx.enter_context(nc.psum_tensor(name + "psB", [128, 512], F32))
        names = ("waited", "edges_in", "edges_used", "slots_free", "spread_ready", "spread_free", "targets_ready", "ends_ready",
                 "ends_turned", "carry_ready", "carry_turned", "diff_ready", "weights_done", "values_ready",
                 "sums_done", "sums_free", "merge_ready", "merge_done", "pe_waited", "consts")
        S = {n: sem(n) for n in names}
        gathered = [sem(f"gathered{b}") for b in range(NG)]
        n_in = 4 if gat else 3
        block = ctx.enter_context(nc.Block())

        @block.sync
        def _(sp):
            if gat:
                sp.dma_start(wed[:].rearrange("p a f -> p (a f)"), a["L0_gnn_W_edge"].rearrange("a f -> (a f)").partition_broadcast(128)).then_inc(S["consts"], 16)
                sp.dma_start(atte[:], a["L0_gnn_att_edge"].rearrange("h c -> (h c)").partition_broadcast(128)).then_inc(S["consts"], 16)
            bufs = [(src, "src_p"), (dst3, "dst_p"), (dstb, "dst_all")]
            if gat:
                bufs.append((attr[:].rearrange("p t c -> p (t c)"), "attr_p"))
            load_steps(nc, sp, g, a, bufs, S["edges_in"],
                       (None, [(gathered[-1], 16 * len(BATCH[-1])), (S["edges_used"], 1)]))

        @block.gpsimd
        def _(pool):
            with pool.Fori(0, g["n_steps"](pool)) as s:
                pool.wait_ge(S["edges_in"], s * (16 * n_in) + 16 * n_in)
                for b, tiles in enumerate(BATCH):
                    pool.wait_ge(S["slots_free"], s * NG + b + 1)
                    pool.sem_inc(S["waited"], 1)
                    for t in tiles:
                        nc.gpsimd.indirect_dma_start(
                            out=G[:, t, 0:width], out_offset=None, in_=table,
                            in_offset=bass.IndirectOffsetOnAxis(ap=src[:, t:t + 1], axis=0)).then_inc(gathered[b], 16)

        @block.tensor
        def _(pe):
            pe.sem_inc(S["slots_free"], NG)
            with pe.Fori(0, g["n_steps"](pe)) as s:
                blk = pe.value_load(g["steps_i"][0:1, bass.ds(s, 1)], min_val=0, max_val=NB - 1)
                pe.wait_ge(S["targets_ready"], s + 1)
                onehot = OT[:].rearrange("d (p t) -> d t p", t=T)
                for b, tiles in enumerate(BATCH):
                    pe.wait_ge(S["spread_free"], s * NG + b + 1)
                    for i, t in enumerate(tiles):
                        mmi = nc.tensor.matmul(psQ[:, b % 3, i * QW:(i + 1) * QW], onehot[:, t, :],
                                               Q[:, bass.ds(blk, 1), 0:QW].rearrange("p a f -> p (a f)"), start=True, stop=True)
                    mmi.then_inc(S["spread_ready"], 1)
                pe.wait_ge(S["ends_ready"], s + 1)
                for k in range(6):
                    mmi = nc.tensor.transpose(psT[0:H, k // 4, (k % 4) * 128:(k % 4 + 1) * 128], TI[:, k, :], g["eye"][:])
                mmi.then_inc(S["ends_turned"], 1)
                pe.wait_ge(S["carry_ready"], s + 1)
                pe.sem_inc(S["pe_waited"], 1)
                for k in range(2):
                    mmi = nc.tensor.transpose(psB[:, k * H:(k + 1) * H], LR[:, k, :], g["eye"][0:H, 0:H])
                mmi.then_inc(S["carry_turned"], 1)
                pe.wait_ge(S["sums_free"], s + 1)
                for b, tiles in enumerate(BATCH):
                    pe.wait_ge(S["values_ready"], s * NG + b + 1)
                    for t in tiles:
                        mmi = nc.tensor.matmul(psA[0:BN, 0:NC], O[:, t, :], G[:, t, vo:vo + NC],
                                               start=(t == 0), stop=(t == T - 1))
                    if b < NG - 1:
                        mmi.then_inc(S["slots_free"], 1)
                mmi.then_inc(S["sums_done"], 1)
                pe.wait_ge(S["sums_done"], s + 1)
                pe.sem_inc(S["slots_free"], 1)

        @block.scalar
        def _(act):
            with act.Fori(0, g["n_steps"](act)) as s:
                act.wait_ge(S["diff_ready"], s + 1)
                nc.scalar.activation(G[:, :, wo:wo + H].rearrange("p t h -> p h t"), A[:], ACT.Exp).then_inc(S["weights_done"], 1)
                act.wait_ge(S["merge_ready"], s + 1)
                nc.scalar.activation(ex[:], mm[:, 0:2 * H], ACT.Exp).then_inc(S["merge_done"], 1)

        @block.vector
        def _(dve):
            def bc(x, shape):
                return x.broadcast_to(shape)

            V = nc.vector
            if gat:
                dve.wait_ge(S["consts"], 32)
                V.tensor_tensor(wed[:], wed[:], bc(atte[:].unsqueeze(1), [128, 13, D]), ALU.mult)
                dve.drain()
                V.tensor_reduce(we[:].rearrange("p h k -> p k h"), wed[:].rearrange("p k (h c) -> p k h c", h=4), AX.X, ALU.add)
                V.memset(G[:, :, GW - 1:GW], 1.0)
            V.memset(ST[:], 0.0)
            V.memset(LR[:], -BIG)
            V.memset(Rf[:, :, 0:1], -BIG)
            V.memset(Rb[:, :, T - 1:T], -BIG)
            dve.drain()
            dve.sem_inc(S["spread_free"], 3)
            dve.sem_inc(S["sums_free"], 1)
            with dve.Fori(0, g["n_steps"](dve)) as s:
                blk = dve.value_load(g["steps_i"][0:1, bass.ds(s, 1)], min_val=0, max_val=NB - 1)
                sc = bass.ds(s, 1)
                dve.wait_ge(S["edges_in"], s * (16 * n_in) + 16 * n_in)
                V.tensor_scalar(dstf[:], dst3[:], g["base_t"][:, sc], None, ALU.subtract)
                V.tensor_scalar(OT[:], dstb[:], g["basep_t"][0:BN, sc], None, ALU.is_equal)
                dve.drain()
                V.tensor_tensor(O[:], bc(g["iota"][:, 0:BN].unsqueeze(1), [128, T, BN]),
                                bc(dstf[:, 1:T + 1].unsqueeze(2), [128, T, BN]), ALU.is_equal).then_inc(S["targets_ready"], 1)
                V.tensor_tensor(ne[:], dstf[:, 1:T + 2], dstf[:, 0:T + 1], ALU.not_equal)
                V.tensor_scalar(hm[:], dstf[:, 1:T + 1], dstf[:, 1:2], -BIG, ALU.not_equal, ALU.mult)
                V.tensor_scalar(tm[:], dstf[:, 1:T + 1], dstf[:, T:T + 1], -BIG, ALU.not_equal, ALU.mult)
                dve.drain()
                V.memset(ne[0:1, 0:1], 1.0)
                dve.drain()
                V.tensor_scalar(rb[:], ne[:], -BIG, None, ALU.mult)
                dve.drain()
                V.tensor_copy(Rf[:, :, 1:T], bc(rb[:, 1:T].unsqueeze(1), [128, H, T - 1]))
                V.tensor_copy(Rb[:, :, 0:T - 1], bc(rb[:, 1:T].unsqueeze(1), [128, H, T - 1]))
                if gat:
                    for h in range(4):
                        V.tensor_tensor(pr[:], attr[:], bc(we[:, h:h + 1, :], [128, T, 13]), ALU.mult)
                        dve.drain()
                        V.tensor_reduce(G[:, :, GW - 5 + h:GW - 4 + h].rearrange("p t a -> p (t a)"), pr[:], AX.X, ALU.add)
                        dve.drain()
                V.memset(X1[:], 0.0).then_inc(S["edges_used"], 1)
                for b, tiles in enumerate(BATCH):
                    n = len(tiles)
                    t0, t1 = tiles[0], tiles[-1] + 1
                    dve.wait_ge(gathered[b], s * (16 * n) + 16 * n)
                    dve.wait_ge(S["spread_ready"], s * NG + b + 1)
                    q = psQ[:, b % 3, 0:n * QW].rearrange("p (t f) -> p t f", f=QW)
                    if gat:
                        V.tensor_tensor(A[:, :, t0:t1].rearrange("p h t -> p t h"), q, G[:, t0:t1, 0:4], ALU.add).then_inc(S["spread_free"], 1)
                    else:
                        V.tensor_tensor(G[:, t0:t1, 0:D], q, G[:, t0:t1, 0:D], ALU.mult).then_inc(S["spread_free"], 1)
                        dve.drain()
                        V.tensor_reduce(A[:, :, t0:t1].rearrange("p h t -> p t h"),
                                        G[:, t0:t1, 0:D].rearrange("p t (h c) -> p t h c", h=H), AX.X, ALU.add)
                dve.drain()
                if gat:
                    V.tensor_tensor(A[:], A[:], G[:, :, GW - 5:GW - 1].rearrange("p t h -> p h t"), ALU.add)
                    dve.drain()
                    V.scalar_tensor_tensor(out=A[:], in0=A[:], scalar=0.2, in1=A[:], op0=ALU.mult, op1=ALU.max)
                    dve.drain()
                fl = lambda x: x[:].rearrange("p h t -> p (h t)")
                V.tensor_tensor_scan(fl(Fw), fl(Rf), fl(A), -BIG, ALU.add, ALU.max)
                dve.drain()
                V.tensor_tensor_scan(fl(M)[:, ::-1], fl(Rb)[:, ::-1], fl(Fw)[:, ::-1], -BIG, ALU.add, ALU.max)
                dve.drain()
                V.tensor_copy(TI[:, 0, :], Fw[:, :, T - 1])
                V.tensor_copy(TI[:, 1, :], M[:, :, 0])
                V.tensor_tensor(TI[:, 2, :], bc(hm[:, T - 1:T], [128, H]), bc(rb[:, 0:1], [128, H]), ALU.min)
                V.tensor_tensor(TI[:, 3, :], bc(hm[:, T - 1:T], [128, H]), bc(rb[:, T:T + 1], [128, H]), ALU.min)
                V.tensor_copy(TI[:, 4, :], bc(rb[:, 0:1], [128, H]))
                V.tensor_copy(TI[:, 5, :], bc(rb[:, T:T + 1], [128, H])).then_inc(S["ends_ready"], 1)
                dve.wait_ge(S["ends_turned"], s + 1)
                V.tensor_copy(TS[:].rearrange("h k p -> h (k p)"), psT[0:H, :, :].rearrange("h a b -> h (a b)")[:, 0:768])
                dve.drain()
                V.tensor_tensor_scan(UV[:, 0, :], TS[:, 2, :], TS[:, 0, :], -BIG, ALU.add, ALU.max)
                V.tensor_tensor_scan(UV[:, 1, ::-1], TS[:, 3, ::-1], TS[:, 1, ::-1], -BIG, ALU.add, ALU.max)
                dve.drain()
                V.tensor_tensor(LR[:, 0, 1:128], UV[:, 0, 0:127], TS[:, 4, 1:128], ALU.add)
                V.tensor_tensor(LR[:, 1, 0:127], UV[:, 1, 1:128], TS[:, 5, 0:127], ALU.add).then_inc(S["carry_ready"], 1)
                dve.wait_ge(S["carry_turned"], s + 1)
                for k, mask in ((0, hm), (1, tm)):
                    V.tensor_tensor(X1[:], bc(psB[:, k * H:(k + 1) * H].unsqueeze(2), [128, H, T]),
                                    bc(mask[:].unsqueeze(1), [128, H, T]), ALU.add)
                    dve.drain()
                    V.tensor_tensor(M[:], M[:], X1[:], ALU.max)
                    dve.drain()
                V.tensor_tensor(A[:], A[:], M[:], ALU.subtract).then_inc(S["diff_ready"], 1)
                V.tensor_tensor(G[:, :, mo:mo + H].rearrange("p t h -> p h t"), M[:], bc(ne[:, 0:T].unsqueeze(1), [128, H, T]), ALU.mult)
                V.tensor_copy(G[:, :, fo:fo + 1].rearrange("p t a -> p (t a)"), ne[:, 0:T])
                dve.wait_ge(S["weights_done"], s + 1)
                for b, tiles in enumerate(BATCH):
                    t0, t1 = tiles[0], tiles[-1] + 1
                    v = G[:, t0:t1, vo:vo + D].rearrange("p t (h c) -> p t h c", h=H)
                    V.tensor_tensor(v, v, bc(G[:, t0:t1, wo:wo + H].unsqueeze(3), [128, t1 - t0, H, C]), ALU.mult).then_inc(S["values_ready"], 1)
                dve.wait_ge(S["sums_done"], s + 1)
                V.tensor_copy(acc[:], psA[0:BN, 0:NC]).then_inc(S["sums_free"], 1)
                dve.drain()
                V.tensor_scalar(mm[:, 2 * H:2 * H + 1], acc[:, D + 2 * H:D + 2 * H + 1], BIG, -BIG, ALU.mult, ALU.add)
                dve.drain()
                V.tensor_scalar(mm[:, H:2 * H], acc[:, D + H:D + 2 * H], mm[:, 2 * H:2 * H + 1], None, ALU.add)
                V.tensor_scalar(mm[:, 0:H], ST[:, D + H:D + 2 * H], g["neg_t"][0:BN, sc], None, ALU.add)
                dve.drain()
                V.tensor_tensor(ST[:, D + H:D + 2 * H], mm[:, 0:H], mm[:, H:2 * H], ALU.max)
                dve.drain()
                V.tensor_tensor(mm[:, 0:2 * H].rearrange("p (k h) -> p k h", k=2), mm[:, 0:2 * H].rearrange("p (k h) -> p k h", k=2),
                                bc(ST[:, D + H:D + 2 * H].unsqueeze(1), [BN, 2, H]), ALU.subtract).then_inc(S["merge_ready"], 1)
                dve.wait_ge(S["merge_done"], s + 1)
                for x, k in ((ST, 0), (acc, 1)):
                    xv = x[:, 0:D].rearrange("p (h c) -> p h c", h=H)
                    V.tensor_tensor(xv, xv, bc(ex[:, k * H:(k + 1) * H].unsqueeze(2), [BN, H, C]), ALU.mult)
                    V.tensor_tensor(x[:, D:D + H], x[:, D:D + H], ex[:, k * H:(k + 1) * H], ALU.mult)
                dve.drain()
                V.tensor_tensor(ST[:, 0:D + H], ST[:, 0:D + H], acc[:, 0:D + H], ALU.add)
                if gat:
                    V.scalar_tensor_tensor(out=ST[:, NC - 5:NC], in0=ST[:, NC - 5:NC], scalar=g["keep_t"][0:BN, sc],
                                           in1=acc[:, NC - 5:NC], op0=ALU.mult, op1=ALU.add)
                dve.drain()
                V.tensor_copy(RES[:, bass.ds(blk, 1), 0:NC].rearrange("p a f -> p (a f)"), ST[:])
            dve.drain()


def count_neighbours(g):
    nc, a, deg, eye, iota, counts, more_i, steps_i = (
        g[k] for k in ("nc", "a", "deg", "eye", "iota", "counts", "more_i", "steps_i"))
    GROUP = 4
    groups = [list(range(b, min(b + GROUP, NB))) for b in range(0, NB, GROUP)]
    chunks = [list(range(p, min(p + CB, PAIRS))) for p in range(0, PAIRS, CB)]
    with ExitStack() as ctx:
        sb = lambda n, s, dt=F32: ctx.enter_context(nc.sbuf_tensor("cn" + n, s, dt))
        sem = phase_semaphores(nc, ctx, "cn")
        tri = sb("tri", [BN, BN])
        ones = sb("ones", [BN, BN])
        cum = sb("cum", [1, 3, NB])
        top = sb("top", [BN, 1])
        big = sb("big", [1, 4])
        start = sb("start", [BN, NB])
        startp = sb("startp", [PAIRS, NB, 2], I32)
        degp = sb("degp", [PAIRS, NB, 2])
        raw = sb("raw", [PAIRS, NB, 2, SLOTS], I32)
        lo = sb("lo", [PAIRS, NB, 2, SLOTS])
        hi = sb("hi", [PAIRS, NB, 2, SLOTS])
        valid = sb("valid", [PAIRS, NB, 2, SLOTS])
        LH = sb("LH", [128, NB, 2, PAIRS], F16)
        iol = sb("iol", [128, BN], F16)
        ioh = sb("ioh", [128, 2 * NB], F16)
        L = sb("L", [128, 2, PAIRS, BN], F16)
        K = sb("K", [128, 2, PAIRS, 2 * NB], F16)
        CO = sb("CO", [BN, 2, NB, BN])
        ps = ctx.enter_context(nc.psum_tensor("cnps", [128, BANKS, 512], F32))
        psT = ctx.enter_context(nc.psum_tensor("cnpsT", [128, 512], F32))
        S = {n: sem(n) for n in ("ready", "totalled", "summed", "started", "paired", "starts_known", "tabled", "turned", "turned_out",
                                 "places_ready", "blocks_ready", "counted", "copied", "waited")}
        stored = [sem(f"stored{u}") for u in range(2)]
        fetched = [sem(f"fetched{k}") for k in range(len(groups))]
        block = ctx.enter_context(nc.Block())

        @block.gpsimd
        def _(pool):
            pool.wait_ge(S["starts_known"], 1)
            src_flat = a["src_p"].rearrange("(e a) -> e a", a=1)
            for k, blocks in enumerate(groups):
                for b in blocks:
                    for h in range(2):
                        nc.gpsimd.indirect_dma_start(
                            out=raw[:, b, h, :], out_offset=None, in_=src_flat,
                            in_offset=bass.IndirectOffsetOnAxis(ap=startp[:, b, h:h + 1], axis=0)).then_inc(fetched[k], 16)

        @block.vector
        def _(dve):
            V = nc.vector
            dr = dve.drain
            V.memset(ones[:], 1.0)
            V.memset(raw[:].rearrange("p b a j -> p (b a j)")[:, 0:1], 0)
            V.memset(degp[:], 0.0)
            V.memset(startp[:], 0)
            V.tensor_scalar(tri[:], iota[0:BN, 0:BN], g["iota_p"][0:BN, 0:1], None, ALU.is_gt)
            V.tensor_scalar(iol[:], iota[:, 0:BN], 1.0, None, ALU.add)
            V.tensor_copy(ioh[:], iota[:, 0:2 * NB])
            V.tensor_reduce(top[:], deg[:], AX.X, ALU.max).then_inc(S["ready"], 1)
            dve.wait_ge(S["totalled"], 1)
            V.tensor_copy(cum[:, 0, :], psT[0:1, 0:NB])
            V.tensor_reduce(big[:, 0:1], psT[0:1, NB:NB + BN], AX.X, ALU.max)
            V.memset(big[:, 3:4], 0.0)
            V.tensor_scalar(cum[:, 2, :], psT[0:1, 0:NB], 0.0, None, ALU.mult)
            dr()
            V.tensor_tensor_scan(cum[:, 1, :], cum[:, 0, :], cum[:, 2, :], 0.0, ALU.add, ALU.add)
            V.tensor_scalar(big[:, 1:2], big[:, 0:1], float(SLOTS), None, ALU.is_gt)
            V.tensor_copy(big[:, 2:3], steps_i[:, 2 * SMAX:2 * SMAX + 1])
            dr()
            V.tensor_tensor(big[:, 1:2], big[:, 1:2], big[:, 2:3], ALU.mult)
            V.tensor_tensor(cum[:, 2, :], cum[:, 1, :], cum[:, 0, :], ALU.subtract).then_inc(S["summed"], 1)
            dr()
            V.tensor_copy(more_i[:], big[:, 1:2])
            dve.wait_ge(S["started"], 1)
            V.tensor_copy(start[:], psT[0:BN, 256:256 + NB]).then_inc(S["ready"], 1)
            dve.wait_ge(S["paired"], 1)
            for h in range(2):
                n = PAIRS - h
                V.tensor_copy(startp[0:n, :, h], psT[0:n, h * 64:h * 64 + NB])
                V.tensor_copy(degp[0:n, :, h], psT[0:n, h * 64 + NB:h * 64 + 2 * NB])
            dr()
            V.memset(top[:], 0.0).then_inc(S["starts_known"], 1)
            for k, blocks in enumerate(groups):
                b0, n = blocks[0], len(blocks)
                x, l, h, v = (q[:, b0:b0 + n] for q in (raw, lo, hi, valid))
                shape = [PAIRS, n, 2, SLOTS]
                V.tensor_tensor(v, iota[0:PAIRS, 0:SLOTS].unsqueeze(1).unsqueeze(1).broadcast_to(shape),
                                degp[:, b0:b0 + n, :].unsqueeze(3).broadcast_to(shape), ALU.is_lt)
                dve.wait_ge(fetched[k], 32 * n)
                V.tensor_copy(l, x)
                dr()
                V.tensor_scalar(h, l, -float(BN // 2), 1.0 / BN, ALU.add, ALU.mult)
                dr()
                V.tensor_scalar(h, h, ROUND, None, ALU.add)
                dr()
                V.tensor_scalar(h, h, -ROUND, None, ALU.add)
                dr()
                V.scalar_tensor_tensor(out=l, in0=h, scalar=-float(BN), in1=l, op0=ALU.mult, op1=ALU.add)
                dr()
                V.scalar_tensor_tensor(out=l, in0=l, scalar=1.0, in1=v, op0=ALU.add, op1=ALU.mult)
                V.tensor_scalar(h[:, :, 1, :], h[:, :, 1, :], float(NB), None, ALU.add)
                dr()
                V.memset(top[:], 0.0).then_inc(S["tabled"], 1)
            dve.sem_inc(S["counted"], 2 * BANKS)
            dve.sem_inc(S["copied"], BANKS)
            for u in range(2):
                dve.sem_inc(stored[u], 16)
            dve.wait_ge(S["turned_out"], len(groups))
            with dve.Fori(0, NB // 2) as i:
                for u in range(2):
                    dve.wait_ge(S["counted"], (i * 2 + u) * BANKS + BANKS)
                    for c, pairs in enumerate(chunks):
                        p0, n = pairs[0], len(pairs)
                        lb, hb = (LH[:, bass.ds(i * 2 + u, 1), k, p0:p0 + n].rearrange("p a n -> p (a n)") for k in range(2))
                        V.tensor_tensor(K[:, u, p0:p0 + n, :], ioh[:].unsqueeze(1).broadcast_to([128, n, 2 * NB]),
                                        hb.unsqueeze(2).broadcast_to([128, n, 2 * NB]), ALU.is_equal).then_inc(S["blocks_ready"], 1)
                        V.tensor_tensor(L[:, u, p0:p0 + n, :], iol[:].unsqueeze(1).broadcast_to([128, n, BN]),
                                        lb.unsqueeze(2).broadcast_to([128, n, BN]), ALU.is_equal).then_inc(S["places_ready"], 1)

        @block.tensor
        def _(pe):
            pe.wait_ge(S["ready"], 1)
            nc.tensor.matmul(psT[0:1, 0:NB], ones[:, 0:1], deg[:], start=True, stop=True)
            nc.tensor.matmul(psT[0:1, NB:NB + BN], top[:], eye[0:BN, 0:BN], start=True, stop=True).then_inc(S["totalled"], 1)
            pe.wait_ge(S["summed"], 1)
            nc.tensor.matmul(psT[0:BN, 256:256 + NB], tri[:], deg[:], start=True, stop=False)
            nc.tensor.matmul(psT[0:BN, 256:256 + NB], ones[0:1, :], cum[:, 2, :], start=False, stop=True).then_inc(S["started"], 1)
            pe.wait_ge(S["ready"], 2)
            for h in range(2):
                n = PAIRS - h
                pick = eye[0:BN, h:BN:2]
                nc.tensor.matmul(psT[0:n, h * 64:h * 64 + NB], pick, start[:], start=True, stop=True)
                mmi = nc.tensor.matmul(psT[0:n, h * 64 + NB:h * 64 + 2 * NB], pick, deg[:], start=True, stop=True)
            mmi.then_inc(S["paired"], 1)
            for k, blocks in enumerate(groups):
                pe.wait_ge(S["tabled"], k + 1)
                if k >= 1:
                    pe.wait_ge(S["turned_out"], k)
                for i, b in enumerate(blocks):
                    for h, x in enumerate((lo, hi)):
                        mmi = nc.tensor.transpose(psT[:, (2 * i + h) * PAIRS:(2 * i + h + 1) * PAIRS],
                                                  x[:, b].rearrange("p a j -> p (a j)"), eye[0:PAIRS, 0:PAIRS])
                mmi.then_inc(S["turned"], 1)
            with pe.Fori(0, NB // 2) as i:
                for u in range(2):
                    for c, pairs in enumerate(chunks):
                        k = (i * 2 + u) * BANKS + (c + 1)
                        pe.wait_ge(S["places_ready"], k)
                        pe.wait_ge(S["blocks_ready"], k)
                        pe.wait_ge(S["copied"], k)
                        for j, p in enumerate(pairs):
                            mmi = nc.tensor.matmul(ps[0:BN, c, j * 2 * NB:(j + 1) * 2 * NB], L[:, u, p, :], K[:, u, p, :],
                                                   start=True, stop=True)
                        mmi.then_inc(S["counted"], 1)

        @block.scalar
        def _(act):
            for k, blocks in enumerate(groups):
                act.wait_ge(S["turned"], k + 1)
                n = len(blocks)
                nc.scalar.copy(LH[:, blocks[0]:blocks[0] + n].rearrange("p b h n -> p (b h n)"),
                               psT[:, 0:2 * n * PAIRS]).then_inc(S["turned_out"], 1)
            with act.Fori(0, NB // 2) as i:
                for u in range(2):
                    act.wait_ge(stored[u], i * 16 + 16)
                    for c, pairs in enumerate(chunks):
                        act.wait_ge(S["counted"], (i * 2 + u) * BANKS + (2 * BANKS + c + 1))
                        d0 = 2 * pairs[0]
                        d1 = min(2 * pairs[-1] + 2, BN)
                        nc.scalar.copy(CO[:, u, :, d0:d1].rearrange("p h d -> p d h"),
                                       ps[0:BN, c, 0:(d1 - d0) * NB].rearrange("p (d h) -> p d h", h=NB)).then_inc(S["copied"], 1)

        @block.sync
        def _(sp):
            with sp.Fori(0, NB // 2) as i:
                for u in range(2):
                    sp.wait_ge(S["copied"], (i * 2 + u) * BANKS + 2 * BANKS)
                    sp.sem_inc(S["waited"], 1)
                    sp.dma_start(counts[bass.ds(i * 2 + u, 1)].rearrange("a l n -> (a l) n"),
                                 CO[:, u].rearrange("p h d -> p (h d)")).then_inc(stored[u], 16)
            for u in range(2):
                sp.wait_ge(stored[u], NB // 2 * 16 + 16)


def count_neighbours_any(g):
    nc, a, counts, iota = (g[k] for k in ("nc", "a", "counts", "iota"))
    banks = [list(range(h, min(h + HI, NB))) for h in range(0, NB, HI)]
    with ExitStack() as ctx:
        sb = lambda n, s, dt=F32: ctx.enter_context(nc.sbuf_tensor("ca" + n, s, dt))
        sem = phase_semaphores(nc, ctx, "ca")
        src = sb("src", [128, T], I32)
        dst = sb("dst", [128, T], I32)
        d = sb("d", [128, T])
        out_of = sb("out_of", [128, T])
        lo = sb("lo", [128, T])
        key = sb("key", [128, T])
        keys = sb("keys", [128, NP])
        L = sb("L", [128, BN], F16)
        K = sb("K", [128, NP], F16)
        acc = sb("acc", [BN, NP])
        ps = ctx.enter_context(nc.psum_tensor("caps", [128, HBANKS, 512], F32))
        S = {n: sem(n) for n in ("keys_in", "waited", "edges_in", "hot", "counted", "added", "stored")}
        block = ctx.enter_context(nc.Block())

        def steps(eng):
            return eng.value_load(g["more_i"][:], min_val=0, max_val=SMAX)

        @block.sync
        def _(sp):
            sp.dma_start(keys[:], a["keys"].partition_broadcast(128)).then_inc(S["keys_in"], 16)
            sp.sem_inc(S["added"], 1)
            n = steps(sp)
            with sp.If(n > 0), sp.Fori(0, n) as s:
                e = sp.value_load(g["steps_i"][0:1, bass.ds(s + SMAX, 1)], min_val=0, max_val=E)
                blk = sp.value_load(g["steps_i"][0:1, bass.ds(s, 1)], min_val=0, max_val=NB - 1)
                sp.wait_ge(S["added"], s + 1)
                sp.sem_inc(S["waited"], 1)
                sp.dma_start(src[:], a["src_p"][bass.ds(e, CH)].rearrange("(p t) -> p t", p=128)).then_inc(S["edges_in"], 16)
                sp.dma_start(dst[:], a["dst_p"][bass.ds(e + 1, CH)].rearrange("(p t) -> p t", p=128)).then_inc(S["edges_in"], 16)
                sp.wait_ge(S["added"], s + 2)
                sp.sem_inc(S["waited"], 1)
                sp.dma_start(counts[bass.ds(blk, 1)].rearrange("a l n -> (a l) n"), acc[:]).then_inc(S["stored"], 16)
                sp.wait_ge(S["stored"], s * 16 + 16)
                sp.sem_inc(S["edges_in"], 1)

        @block.vector
        def _(dve):
            V = nc.vector
            dr = dve.drain
            dve.wait_ge(S["keys_in"], 16)
            V.memset(acc[:], 0.0)
            dr()
            n = steps(dve)
            with dve.If(n > 0), dve.Fori(0, n) as s:
                sc = bass.ds(s, 1)
                dve.wait_ge(S["edges_in"], s * 33 + 32)
                V.tensor_scalar(d[:], dst[:], g["base_t"][:, sc], None, ALU.subtract)
                V.tensor_copy(lo[:], src[:])
                dr()
                V.tensor_scalar(key[:], lo[:], -float(BN // 2), 1.0 / BN, ALU.add, ALU.mult)
                V.tensor_scalar(out_of[:], d[:], 0.0, -BIG, ALU.is_lt, ALU.mult)
                dr()
                V.tensor_scalar(key[:], key[:], ROUND, None, ALU.add)
                V.scalar_tensor_tensor(out=d[:], in0=out_of[:], scalar=1.0, in1=d[:], op0=ALU.mult, op1=ALU.add)
                dr()
                V.tensor_scalar(key[:], key[:], -ROUND, None, ALU.add)
                V.tensor_scalar(out_of[:], d[:], float(BN), -BIG, ALU.is_ge, ALU.mult)
                dr()
                V.scalar_tensor_tensor(out=lo[:], in0=key[:], scalar=-float(BN), in1=lo[:], op0=ALU.mult, op1=ALU.add)
                V.tensor_tensor(d[:], d[:], out_of[:], ALU.add)
                dr()
                V.scalar_tensor_tensor(out=key[:], in0=key[:], scalar=float(BN), in1=d[:], op0=ALU.mult, op1=ALU.add)
                dr()
                for t in range(T):
                    if t:
                        dve.wait_ge(S["counted"], s * T + t)
                    V.tensor_scalar(L[:], iota[:, 0:BN], lo[:, t:t + 1], None, ALU.is_equal)
                    V.tensor_scalar(K[:], keys[:], key[:, t:t + 1], None, ALU.is_equal)
                    dr()
                    V.memset(out_of[:], 0.0).then_inc(S["hot"], 1)
                dve.wait_ge(S["counted"], s * T + T)
                for k, his in enumerate(banks):
                    c = slice(his[0] * BN, (his[-1] + 1) * BN)
                    V.scalar_tensor_tensor(out=acc[:, c], in0=acc[:, c], scalar=g["keep_t"][0:BN, sc],
                                           in1=ps[0:BN, k, 0:len(his) * BN], op0=ALU.mult, op1=ALU.add)
                dr()
                V.memset(out_of[:], 0.0).then_inc(S["added"], 1)

        @block.tensor
        def _(pe):
            n = steps(pe)
            with pe.If(n > 0), pe.Fori(0, n) as s:
                for t in range(T):
                    pe.wait_ge(S["hot"], s * T + t + 1)
                    for k, his in enumerate(banks):
                        mmi = nc.tensor.matmul(ps[0:BN, k, 0:len(his) * BN], L[:], K[:, his[0] * BN:(his[-1] + 1) * BN],
                                               start=(t == 0), stop=(t == T - 1))
                    mmi.then_inc(S["counted"], 1)


def dense_sum(g, name):
    nc, RES, SKIP, counts = (g[k] for k in ("nc", "RES", "SKIP", "counts"))
    with ExitStack() as ctx:
        sem = phase_semaphores(nc, ctx, name)
        C = ctx.enter_context(nc.sbuf_tensor(name + "C", [BN, 2, NB, BN], F32))
        ps = ctx.enter_context(nc.psum_tensor(name + "ps", [128, 2, 512], F32))
        S = {n: sem(n) for n in ("waited", "summed", "taken")}
        counts_in = [sem(f"counts_in{u}") for u in range(2)]
        block = ctx.enter_context(nc.Block())

        @block.sync
        def _(sp):
            with sp.Fori(0, NB // 2) as i:
                for u in range(2):
                    sp.wait_ge(S["summed"], i * 2 + u + 1)
                    sp.sem_inc(S["waited"], 1)
                    sp.dma_start(C[:, u].rearrange("p h d -> p (h d)"),
                                 counts[bass.ds(i * 2 + u, 1)].rearrange("a l n -> (a l) n")).then_inc(counts_in[u], 16)

        @block.tensor
        def _(pe):
            pe.sem_inc(S["summed"], 2)
            with pe.Fori(0, NB // 2) as i:
                for u in range(2):
                    pe.wait_ge(counts_in[u], i * 16 + 16)
                    pe.wait_ge(S["taken"], i * 2 + u + 1)
                    for h in range(NB):
                        mmi = nc.tensor.matmul(ps[0:BN, u, 0:D], C[:, u, h, :], SKIP[:, h, :], start=(h == 0), stop=(h == NB - 1))
                    mmi.then_inc(S["summed"], 1)

        @block.vector
        def _(dve):
            dve.sem_inc(S["taken"], 2)
            with dve.Fori(0, NB // 2) as i:
                for u in range(2):
                    dve.wait_ge(S["summed"], i * 2 + u + 3)
                    nc.vector.tensor_copy(RES[:, bass.ds(i * 2 + u, 1), 0:D].rearrange("p a f -> p (a f)"),
                                          ps[0:BN, u, 0:D]).then_inc(S["taken"], 1)
            dve.drain()


def tile_tables(g):
    nc, a, eye, wide_i = (g[k] for k in ("nc", "a", "eye", "wide_i"))
    with ExitStack() as ctx:
        sb = lambda n, s, dt=F32: ctx.enter_context(nc.sbuf_tensor("tt" + n, s, dt))
        sem = phase_semaphores(nc, ctx, "tt")
        dst = sb("dst", [128, NT], I32)
        first = sb("first", [128, NT], I32)
        w = sb("w", [128, NT])
        real = sb("real", [128, NT])
        top = sb("top", [128, 1])
        one = sb("one", [1, 1])
        ps = ctx.enter_context(nc.psum_tensor("ttps", [128, 512], F32))
        loaded, reduced, turned = (sem(n) for n in ("loaded", "reduced", "turned"))
        block = ctx.enter_context(nc.Block())

        @block.sync
        def _(sp):
            sp.dma_start(dst[:], a["dst_cols"]).then_inc(loaded, 16)
            sp.dma_start(first[:], a["dst_cols"][0, :].partition_broadcast(128)).then_inc(loaded, 16)

        @block.vector
        def _(dve):
            V = nc.vector
            dve.wait_ge(loaded, 32)
            node_in_window(nc, w, dst, first)
            dve.drain()
            V.tensor_scalar(real[:], w[:], float(2 * NP), None, ALU.is_lt)
            dve.drain()
            V.tensor_tensor(w[:], w[:], real[:], ALU.mult)
            dve.drain()
            V.tensor_reduce(top[:], w[:], AX.X, ALU.max).then_inc(reduced, 1)
            dve.wait_ge(turned, 1)
            V.tensor_reduce(one[:], ps[0:1, 0:128], AX.X, ALU.max)
            dve.drain()
            V.tensor_scalar(wide_i[:], one[:], float(WIN), None, ALU.is_ge)
            dve.drain()

        @block.tensor
        def _(pe):
            pe.wait_ge(reduced, 1)
            nc.tensor.matmul(ps[0:1, 0:128], top[:], eye[:], start=True, stop=True).then_inc(turned, 1)


def node_in_window(nc, w, dst, first):
    v = lambda x: x[:, 0:NT].rearrange("p (g t) -> p g t", t=GT)
    for tiles in TB:
        t0, n = tiles[0], len(tiles)
        nc.vector.tensor_tensor(v(w)[:, :, t0:t0 + n], v(dst)[:, :, t0:t0 + n],
                                v(first)[:, :, t0:t0 + 1].broadcast_to([128, NT // GT, n]), ALU.subtract)


def relation_tiles(g, name, table):
    nc, a, RES, X, iota, eye = (g[k] for k in ("nc", "a", "RES", "X", "iota", "eye"))
    NBAS = 8
    NGR = NT // GT
    with ExitStack() as ctx:
        sb = lambda n, s, dt=F32: ctx.enter_context(nc.sbuf_tensor(name + n, s, dt))
        sem = phase_semaphores(nc, ctx, name)
        G = sb("G", [128, 2, GT, D])
        idx = sb("idx", [128, 2, GT], I32)
        dst = sb("dst", [128, NT], I32)
        first = sb("first", [128, NT], I32)
        w = sb("w", [128, NT + GT])
        wgt = sb("wgt", [128, NT + GT])
        typ = g["Q"][0:64].bitcast(I32).rearrange("p b f -> p (b f)")[:, 0:2 * GT * 128].rearrange("p (u e) -> p u e", u=2)
        tyo = g["SKIP"][0:64].rearrange("p b f -> p (b f)")[:, 0:GT * 128]
        wc = sb("wc", [64, NBAS])
        coef = sb("coef", [128, 2, GT, NBAS])
        OW = sb("OW", [128, 2, GT, WIN])
        CO = sb("CO", [128, 2, TBMAX, WIN, NBAS])
        AT = sb("AT", [128, NP + WIN, NBAS])
        bases = sb("bases", [D, NBAS, D])
        loopw = sb("loopw", [D, D])
        xT = sb("xT", [D, 2, BN])
        psW = ctx.enter_context(nc.psum_tensor(name + "psW", [128, 2, 512], F32))
        psC = ctx.enter_context(nc.psum_tensor(name + "psC", [128, 512], F32))
        psX = ctx.enter_context(nc.psum_tensor(name + "psX", [128, 2, 512], F32))
        psR = ctx.enter_context(nc.psum_tensor(name + "psR", [128, 2, 512], F32))
        S = {n: sem(n) for n in ("consts", "waited", "types_ready", "coef_made", "coef_used", "products_ready", "summed",
                                 "slots_free", "added", "x_turned", "x_copied", "rows_done", "rows_used")}
        sources_in = [sem(f"sources_in{u}") for u in range(2)]
        types_in = [sem(f"types_in{u}") for u in range(2)]
        gathered = [[sem(f"gathered{u}{b}") for b in range(len(TB))] for u in range(2)]
        NBT = len(TB)
        block = ctx.enter_context(nc.Block())

        @block.sync
        def _(sp):
            for dst_, src_ in ((dst[:], a["dst_cols"]), (first[:], a["dst_cols"][0, :].partition_broadcast(128)),
                               (wgt[:, 0:NT], a["weight_cols"]), (wc[:], a["L1_gnn_w_comp"]),
                               (bases[:], a["L1_gnn_weight"].rearrange("b i o -> i b o")), (loopw[:], a["L1_gnn_loop_weight"])):
                sp.dma_start(dst_, src_).then_inc(S["consts"], 16)
            sp.dma_start(typ[:, 0, :], a["type_p"][0:GT * 128].partition_broadcast(64)).then_inc(types_in[0], 16)
            with sp.Fori(0, NGR // 2) as i:
                for u in range(2):
                    sp.wait_ge(S["types_ready"], i * 2 + u + 1)
                    sp.wait_ge(S["slots_free"], (i * 2 + u) * NBT + NBT)
                    sp.sem_inc(S["waited"], 1)
                    sp.dma_start(idx[:, u, :], a["src_cols"][:, bass.ds((i * 2 + u) * GT, GT)]).then_inc(sources_in[u], 16)
                    sp.dma_start(typ[:, 1 - u, :], a["type_p"][bass.ds((i * 2 + u + 1) * (GT * 128), GT * 128)].partition_broadcast(64)
                                 ).then_inc(types_in[1 - u], 16)

        @block.gpsimd
        def _(pool):
            with pool.Fori(0, NGR // 2) as i:
                for u in range(2):
                    pool.wait_ge(sources_in[u], i * 16 + 16)
                    for b, tiles in enumerate(TB):
                        pool.wait_ge(S["slots_free"], (i * 2 + u) * NBT + (b + 1))
                        pool.sem_inc(S["waited"], 1)
                        for t in tiles:
                            nc.gpsimd.indirect_dma_start(
                                out=G[:, u, t, :], out_offset=None, in_=table,
                                in_offset=bass.IndirectOffsetOnAxis(ap=idx[:, u, t:t + 1], axis=0)).then_inc(gathered[u][b], 16)

        @block.tensor
        def _(pe):
            pe.sem_inc(S["slots_free"], 2 * NBT)
            pe.wait_ge(S["consts"], 96)
            onehot = tyo[:].rearrange("r (t p) -> r t p", p=128)

            def coefficients():
                for t in range(GT):
                    mmi = nc.tensor.matmul(psC[:, t * NBAS:(t + 1) * NBAS], onehot[:, t, :], wc[:], start=True, stop=True)
                mmi.then_inc(S["coef_made"], 1)

            pe.wait_ge(S["types_ready"], 2)
            coefficients()
            with pe.Fori(0, NGR // 2) as i:
                for u in range(2):
                    for b, tiles in enumerate(TB):
                        k = (i * 2 + u) * NBT + (b + 1)
                        pe.wait_ge(S["products_ready"], k)
                        pe.wait_ge(gathered[u][b], i * (16 * len(tiles)) + 16 * len(tiles))
                        pe.wait_ge(S["added"], k)
                        p = (u * NBT + b) % 2
                        for j, t in enumerate(tiles):
                            mmi = nc.tensor.matmul(psW[:, p, 0:WIN * NBAS], G[:, u, t, :],
                                                   CO[:, p, j].rearrange("p w b -> p (w b)"), start=(j == 0), stop=(t == tiles[-1]))
                        mmi.then_inc(S["summed"], 1)
                        pe.wait_ge(S["summed"], k)
                        pe.sem_inc(S["slots_free"], 1)
                        if b == 0:
                            pe.wait_ge(S["types_ready"], (i * 2 + u) + 3)
                            pe.wait_ge(S["coef_used"], (i * 2 + u) + 1)
                            coefficients()
            for b in range(NB + 1):
                if b < NB:
                    if b >= 2:
                        pe.wait_ge(S["x_copied"], b - 1)
                    nc.tensor.transpose(psX[:, b % 2, 0:BN], X[:, b, :], eye[0:BN, 0:BN]).then_inc(S["x_turned"], 1)
                if b == 0:
                    pe.wait_ge(S["added"], NGR * NBT + 2)
                if b >= 1:
                    c = b - 1
                    pe.wait_ge(S["x_copied"], c + 1)
                    if c >= 2:
                        pe.wait_ge(S["rows_used"], c - 1)
                    for k in range(NBAS):
                        nc.tensor.matmul(psR[0:BN, c % 2, 0:D], AT[:, c * BN:(c + 1) * BN, k], bases[:, k, :], start=(k == 0), stop=False)
                    nc.tensor.matmul(psR[0:BN, c % 2, 0:D], xT[:, c % 2, :], loopw[:], start=False, stop=True).then_inc(S["rows_done"], 1)

        @block.scalar
        def _(act):
            for b in range(NB):
                act.wait_ge(S["x_turned"], b + 1)
                if b >= 2:
                    act.wait_ge(S["rows_done"], b - 1)
                nc.scalar.copy(xT[:, b % 2, :], psX[:, b % 2, 0:BN]).then_inc(S["x_copied"], 1)

        @block.vector
        def _(dve):
            V = nc.vector
            dve.sem_inc(S["types_ready"], 1)
            dve.wait_ge(S["consts"], 96)
            node_in_window(nc, w, dst, first)
            V.memset(w[:, NT:], 0.0)
            V.memset(wgt[:, NT:], 0.0)

            def match_types(u):
                V.tensor_scalar(tyo[:], typ[:, u, :], g["iota_p"][0:64, 0:1], None, ALU.is_equal).then_inc(S["types_ready"], 1)

            def match_targets(u, gt):
                V.tensor_tensor(OW[:, u], iota[:, 0:WIN].unsqueeze(1).broadcast_to([128, GT, WIN]),
                                w[:, gt].unsqueeze(2).broadcast_to([128, GT, WIN]), ALU.is_equal)

            def weigh(u, gt):
                V.tensor_tensor(coef[:, u], psC[:, 0:GT * NBAS].rearrange("p (t b) -> p t b", b=NBAS),
                                wgt[:, gt].unsqueeze(2).broadcast_to([128, GT, NBAS]), ALU.mult).then_inc(S["coef_used"], 1)

            def products(u, b, p):
                t0, n = TB[b][0], len(TB[b])
                V.tensor_tensor(CO[:, p, 0:n], OW[:, u, t0:t0 + n, :].unsqueeze(3).broadcast_to([128, n, WIN, NBAS]),
                                coef[:, u, t0:t0 + n, :].unsqueeze(2).broadcast_to([128, n, WIN, NBAS]),
                                ALU.mult).then_inc(S["products_ready"], 1)

            dve.wait_ge(types_in[0], 16)
            match_types(0)
            dve.drain()
            match_targets(0, slice(0, GT))
            V.memset(AT[:], 0.0)
            dve.wait_ge(S["coef_made"], 1)
            weigh(0, slice(0, GT))
            dve.drain()
            products(0, 0, 0)
            dve.sem_inc(S["added"], 2)
            with dve.Fori(0, NGR // 2) as i:
                for u in range(2):
                    later = bass.ds((i * 2 + u + 1) * GT, GT)
                    dve.wait_ge(types_in[1 - u], i * 16 + (16 + 16 * u))
                    match_types(1 - u)
                    match_targets(1 - u, later)
                    for b, tiles in enumerate(TB):
                        k = (i * 2 + u) * NBT + b
                        p = (u * NBT + b) % 2
                        if b + 1 < NBT:
                            products(u, b + 1, 1 - p)
                        else:
                            products(1 - u, 0, 1 - p)
                        base = dve.value_load(first[0:1, bass.ds((i * 2 + u) * GT + tiles[0], 1)], min_val=0, max_val=N - 1)
                        at = AT[:, bass.ds(base, WIN), :].rearrange("p w b -> p (w b)")
                        dve.wait_ge(S["summed"], k + 1)
                        V.tensor_tensor(at, at, psW[:, p, 0:WIN * NBAS], ALU.add).then_inc(S["added"], 1)
                        if b == 0:
                            dve.wait_ge(S["coef_made"], i * 2 + u + 2)
                            weigh(1 - u, later)
                        dve.drain()
            for b in range(NB):
                dve.wait_ge(S["rows_done"], b + 1)
                V.tensor_copy(RES[:, b, 0:D], psR[0:BN, b % 2, 0:D]).then_inc(S["rows_used"], 1)
            dve.drain()


def relation_pass(g, name, table):
    nc, a, RES, X = (g[k] for k in ("nc", "a", "RES", "X"))
    NBAS = 8
    HB = NBAS // 2
    with ExitStack() as ctx:
        sb = lambda n, s, dt=F32: ctx.enter_context(nc.sbuf_tensor(name + n, s, dt))
        sem = phase_semaphores(nc, ctx, name)
        G = sb("G", [128, T, D])
        src = sb("src", [128, T], I32)
        dst3 = sb("dst3", [128, T + 2], I32)
        wgt = sb("wgt", [128, T])
        typ = sb("typ", [64, CH], I32)
        tyo = sb("tyo", [64, CH])
        wc = sb("wc", [64, NBAS])
        coef = sb("coef", [128, T, NBAS])
        dstf = sb("dstf", [128, T + 2])
        O = sb("O", [128, T, BN])
        CO = sb("CO", [128, 4, NBAS, BN])
        ST = sb("ST", [D, NBAS, BN])
        bases = sb("bases", [D, NBAS, D])
        loopw = sb("loopw", [D, D])
        XB = sb("XB", [BN, D])
        xT = sb("xT", [D, BN])
        psA = ctx.enter_context(nc.psum_tensor(name + "psA", [128, 2, 512], F32))
        psC = ctx.enter_context(nc.psum_tensor(name + "psC", [128, 512], F32))
        psX = ctx.enter_context(nc.psum_tensor(name + "psX", [128, 512], F32))
        psR = ctx.enter_context(nc.psum_tensor(name + "psR", [128, 512], F32))
        S = {n: sem(n) for n in ("consts", "waited", "edges_in", "edges_used", "slots_free", "types_ready", "coef_made", "coef_used", "products_ready",
                                 "products_used", "sums_done", "sums_free", "block_ready", "block_turned", "block_copied", "rows_done",
                                 "rows_used")}
        gathered = [sem(f"gathered{b}") for b in range(NG)]
        block = ctx.enter_context(nc.Block())

        @block.sync
        def _(sp):
            sp.dma_start(wc[:], a["L1_gnn_w_comp"]).then_inc(S["consts"], 16)
            sp.dma_start(bases[:], a["L1_gnn_weight"].rearrange("b i o -> i b o")).then_inc(S["consts"], 16)
            sp.dma_start(loopw[:], a["L1_gnn_loop_weight"]).then_inc(S["consts"], 16)
            with sp.If(g["is_wide"](sp) > 0):
                load_steps(nc, sp, g, a, [(src, "src_p"), (dst3, "dst_p"), (typ, "type_p"), (wgt, "weight_p")], S["edges_in"],
                           (None, [(gathered[-1], 16 * len(BATCH[-1])), (S["edges_used"], 1)]))

        @block.gpsimd
        def _(pool):
            with pool.If(g["is_wide"](pool) > 0), pool.Fori(0, g["n_steps"](pool)) as s:
                pool.wait_ge(S["edges_in"], s * 64 + 64)
                for b, tiles in enumerate(BATCH):
                    pool.wait_ge(S["slots_free"], s * NG + b + 1)
                    pool.sem_inc(S["waited"], 1)
                    for t in tiles:
                        nc.gpsimd.indirect_dma_start(
                            out=G[:, t, :], out_offset=None, in_=table,
                            in_offset=bass.IndirectOffsetOnAxis(ap=src[:, t:t + 1], axis=0)).then_inc(gathered[b], 16)

        @block.tensor
        def _(pe):
            pe.sem_inc(S["slots_free"], NG)
            pe.wait_ge(S["consts"], 48)
            with pe.If(g["is_wide"](pe) > 0), pe.Fori(0, g["n_steps"](pe)) as s:
                pe.wait_ge(S["types_ready"], s + 1)
                onehot = tyo[:].rearrange("r (p t) -> r t p", t=T)
                for t in range(T):
                    mmi = nc.tensor.matmul(psC[:, t * NBAS:(t + 1) * NBAS], onehot[:, t, :], wc[:], start=True, stop=True)
                mmi.then_inc(S["coef_made"], 1)
                pe.wait_ge(S["block_ready"], s + 1)
                nc.tensor.transpose(psX[:, 0:BN], XB[:], g["eye"][0:BN, 0:BN]).then_inc(S["block_turned"], 1)
                pe.wait_ge(S["sums_free"], s + 1)
                for b, tiles in enumerate(BATCH):
                    pe.wait_ge(gathered[b], s * (16 * len(tiles)) + 16 * len(tiles))
                    for t in tiles:
                        pe.wait_ge(S["products_ready"], s * T + t + 1)
                        for k in range(2):
                            mmi = nc.tensor.matmul(psA[:, k, 0:HB * BN], G[:, t, :],
                                                   CO[:, t % 4, k * HB:(k + 1) * HB, :].rearrange("p b d -> p (b d)"),
                                                   start=(t == 0), stop=(t == T - 1))
                        mmi.then_inc(S["products_used"], 1)
                    pe.wait_ge(S["products_used"], s * T + tiles[-1] + 1)
                    pe.sem_inc(S["slots_free"], 1)
                mmi = nc.tensor.matmul(psR[0:1, 0:1], wc[0:1, 0:1], wc[0:1, 0:1], start=True, stop=True)
                mmi.then_inc(S["sums_done"], 1)
                pe.wait_ge(S["block_copied"], s + 1)
                pe.wait_ge(S["rows_used"], s * 2 + 2)
                for k in range(NBAS):
                    nc.tensor.matmul(psR[0:BN, 0:D], ST[:, k, :], bases[:, k, :], start=(k == 0), stop=False)
                nc.tensor.matmul(psR[0:BN, 0:D], xT[:], loopw[:], start=False, stop=True).then_inc(S["rows_done"], 1)

        @block.vector
        def _(dve):
            V = nc.vector
            V.memset(ST[:], 0.0)
            dve.drain()
            dve.sem_inc(S["sums_free"], 1)
            dve.sem_inc(S["rows_used"], 1)
            with dve.If(g["is_wide"](dve) > 0), dve.Fori(0, g["n_steps"](dve)) as s:
                blk = dve.value_load(g["steps_i"][0:1, bass.ds(s, 1)], min_val=0, max_val=NB - 1)
                sc = bass.ds(s, 1)
                dve.wait_ge(S["edges_in"], s * 64 + 64)
                V.tensor_scalar(tyo[:], typ[:], g["iota_p"][0:64, 0:1], None, ALU.is_equal).then_inc(S["types_ready"], 1)
                V.tensor_copy(XB[:], X[:, bass.ds(blk, 1), :].rearrange("p a f -> p (a f)")).then_inc(S["block_ready"], 1)
                V.tensor_scalar(dstf[:], dst3[:], g["base_t"][:, sc], None, ALU.subtract)
                dve.drain()
                V.tensor_tensor(O[:], g["iota"][:, 0:BN].unsqueeze(1).broadcast_to([128, T, BN]),
                                dstf[:, 1:T + 1].unsqueeze(2).broadcast_to([128, T, BN]), ALU.is_equal)
                dve.wait_ge(S["coef_made"], s + 1)
                V.tensor_tensor(coef[:], psC[:, 0:T * NBAS].rearrange("p (t b) -> p t b", b=NBAS),
                                wgt[:].unsqueeze(2).broadcast_to([128, T, NBAS]), ALU.mult).then_inc(S["edges_used"], 1)
                dve.drain()
                for t in range(T):
                    if t >= 4:
                        dve.wait_ge(S["products_used"], s * T + t - 3)
                    V.tensor_tensor(CO[:, t % 4], O[:, t:t + 1, :].broadcast_to([128, NBAS, BN]),
                                    coef[:, t, :].unsqueeze(2).broadcast_to([128, NBAS, BN]), ALU.mult).then_inc(S["products_ready"], 1)
                    if t == 1:
                        dve.wait_ge(S["block_turned"], s + 1)
                        V.tensor_copy(xT[:], psX[:, 0:BN]).then_inc(S["block_copied"], 1)
                dve.wait_ge(S["sums_done"], s + 1)
                V.scalar_tensor_tensor(out=ST[:, 0:HB, :], in0=ST[:, 0:HB, :], scalar=g["keep_t"][:, sc],
                                       in1=psA[:, 0, 0:HB * BN].rearrange("p (b d) -> p b d", d=BN), op0=ALU.mult, op1=ALU.add)
                V.scalar_tensor_tensor(out=ST[:, HB:, :], in0=ST[:, HB:, :], scalar=g["keep_t"][:, sc],
                                       in1=psA[:, 1, 0:HB * BN].rearrange("p (b d) -> p b d", d=BN), op0=ALU.mult, op1=ALU.add)
                dve.drain()
                dve.sem_inc(S["sums_free"], 1)
                dve.sem_inc(S["rows_used"], 1)
                dve.wait_ge(S["rows_done"], s + 1)
                V.tensor_copy(RES[:, bass.ds(blk, 1), 0:D].rearrange("p a f -> p (a f)"), psR[0:BN, 0:D]).then_inc(S["rows_used"], 1)
                dve.drain()


def finish_parts(g, name, work, loads=(), n_sqrt=0, store=None, exps=None):
    nc, a = g["nc"], g["a"]
    with ExitStack() as ctx:
        sb = lambda n, s, dt=F32: ctx.enter_context(nc.sbuf_tensor(name + n, s, dt))
        sem = phase_semaphores(nc, ctx, name)
        mean = sb("mean", [BN, NB])
        var = sb("var", [BN, NB])
        tmp = sb("tmp", [BN, NB, D])
        row = {n: sb(n, [BN, D]) for n in loads}
        sm = sb("sm", [BN, NB, 32])
        loaded, asked, rooted, stored = (sem(n) for n in ("loaded", "asked", "rooted", "stored"))
        block = ctx.enter_context(nc.Block())

        @block.sync
        def _(sp):
            for n in loads:
                sp.dma_start(row[n][:], a[n].partition_broadcast(BN)).then_inc(loaded, 16)
            if store is not None:
                sp.wait_ge(asked, n_sqrt + 1)
                src, dst = store
                sp.dma_start(dst.rearrange("(b p) f -> p b f", p=BN)[:], src[:, 0:NB, :]).then_inc(stored, 16) if N == NP else None
                full = N // BN
                sp.dma_start(dst[0:full * BN].rearrange("(b p) f -> p b f", p=BN), src[:, 0:full, :]).then_inc(stored, 16)
                sp.dma_start(dst[full * BN:N], src[0:N - full * BN, full, :]).then_inc(stored, 16)
                sp.wait_ge(stored, 32)

        @block.scalar
        def _(act):
            k = 0
            if exps:
                act.wait_ge(asked, 1)
                nc.scalar.activation(sm[:, :, 0:exps], sm[:, :, 0:exps], ACT.Exp).then_inc(rooted, 1)
                k = 1
            for i in range(n_sqrt):
                act.wait_ge(asked, k + i + 1)
                nc.scalar.activation(var[:], var[:], ACT.Sqrt).then_inc(rooted, 1)

        @block.vector
        def _(dve):
            dve.wait_ge(loaded, 16 * len(loads)) if loads else None
            work(dve, nc.vector, row, mean, var, tmp, sm, asked, rooted)
            dve.drain()
            nc.vector.memset(sm[:, :, 31:32], 0.0).then_inc(asked, 1)


def rows_of(x):
    return x[:].unsqueeze(1).broadcast_to([BN, NB, D])


def gat_finish(g):
    nc, X, RES, Q, SKIP, cnt1 = (g[k] for k in ("nc", "X", "RES", "Q", "SKIP", "cnt1"))
    H, C = 4, 32

    def work(dve, V, row, mean, var, tmp, sm, asked, rooted):
        dr = dve.drain
        b4 = lambda x: x.broadcast_to([BN, NB, H])
        plain = D + 2 * H + 1
        V.tensor_copy(cnt1[:], RES[:, :, plain + 4])
        V.tensor_copy(g["deg"][:], RES[:, :, plain + 4])
        dr()
        V.tensor_scalar(mean[:], cnt1[:], 1.0, None, ALU.max)
        dr()
        V.reciprocal(mean[:], mean[:])
        dr()
        al = sm[:, :, 8:12]
        V.tensor_tensor(al, RES[:, :, plain:plain + 4], b4(mean[:].unsqueeze(2)), ALU.mult)
        dr()
        V.tensor_tensor(al, al, Q[:, :, 0:4], ALU.add)
        dr()
        V.tensor_tensor(al, al, Q[:, :, 4:8], ALU.add)
        dr()
        V.scalar_tensor_tensor(out=al, in0=al, scalar=0.2, in1=al, op0=ALU.mult, op1=ALU.max)
        dr()
        m = sm[:, :, 12:16]
        V.tensor_tensor(m, RES[:, :, D + H:D + 2 * H], al, ALU.max)
        dr()
        V.tensor_tensor(sm[:, :, 0:4], RES[:, :, D + H:D + 2 * H], m, ALU.subtract)
        V.tensor_tensor(sm[:, :, 4:8], al, m, ALU.subtract)
        dr()
        V.memset(sm[:, :, 30:31], 0.0).then_inc(asked, 1)
        dve.wait_ge(rooted, 1)
        den = sm[:, :, 12:16]
        V.tensor_tensor(den, RES[:, :, D:D + H], sm[:, :, 0:4], ALU.mult)
        dr()
        V.tensor_tensor(den, den, sm[:, :, 4:8], ALU.add)
        dr()
        V.tensor_scalar(den, den, 1e-16, None, ALU.add)
        dr()
        V.reciprocal(den, den)
        dr()
        V.tensor_tensor(sm[:, :, 0:4], sm[:, :, 0:4], den, ALU.mult)
        V.tensor_tensor(sm[:, :, 4:8], sm[:, :, 4:8], den, ALU.mult)
        dr()
        for h in range(H):
            hs = slice(h * C, (h + 1) * C)
            V.tensor_tensor(tmp[:, :, hs], RES[:, :, hs], sm[:, :, h:h + 1].broadcast_to([BN, NB, C]), ALU.mult)
            V.tensor_tensor(SKIP[:, :, hs], SKIP[:, :, hs], sm[:, :, 4 + h:5 + h].broadcast_to([BN, NB, C]), ALU.mult)
        dr()
        y = RES[:, :, 0:D]
        V.tensor_tensor(y, tmp[:], SKIP[:], ALU.add)
        dr()
        V.tensor_tensor(y, y, rows_of(row["L0_gnn_bias"]), ALU.add)
        dr()
        V.tensor_tensor(y, y, X[:], ALU.add)
        dr()
        layernorm(nc, dve, rooted, asked, y, mean, var, tmp, 2)
        V.tensor_tensor(y, y, rows_of(row["L0_gnn_ln_gamma"]), ALU.mult)
        dr()
        V.tensor_tensor(y, y, rows_of(row["L0_gnn_ln_beta"]), ALU.add)
        dr()
        V.scalar_tensor_tensor(out=X[:], in0=y, scalar=0.0, in1=X[:], op0=ALU.max, op1=ALU.add)
        dr()
        layernorm(nc, dve, rooted, asked, X, mean, var, tmp, 3)
        V.tensor_scalar(var[:], cnt1[:], 1.0, None, ALU.add).then_inc(asked, 1)
        dve.wait_ge(rooted, 4)
        V.reciprocal(cnt1[:], var[:])

    finish_parts(g, "f0", work, ("L0_gnn_bias", "L0_gnn_ln_gamma", "L0_gnn_ln_beta"), n_sqrt=3, exps=8)


def relation_finish(g):
    nc, X, RES = (g[k] for k in ("nc", "X", "RES"))

    def work(dve, V, row, mean, var, tmp, sm, asked, rooted):
        y = RES[:, :, 0:D]
        V.tensor_tensor(y, y, rows_of(row["L1_gnn_h_bias"]), ALU.add)
        dve.drain()
        V.scalar_tensor_tensor(out=X[:], in0=y, scalar=0.0, in1=X[:], op0=ALU.max, op1=ALU.add)
        dve.drain()
        layernorm(nc, dve, rooted, asked, X, mean, var, tmp, 1)

    finish_parts(g, "f1", work, ("L1_gnn_h_bias",), n_sqrt=1)


def transformer_finish(g, name, H, last):
    nc, X, RES, SKIP = (g[k] for k in ("nc", "X", "RES", "SKIP"))
    C = D // H

    def work(dve, V, row, mean, var, tmp, sm, asked, rooted):
        den = sm[:, :, 0:H]
        V.tensor_scalar(den, RES[:, :, D:D + H], 1e-16, None, ALU.add)
        dve.drain()
        V.reciprocal(den, den)
        dve.drain()
        y = RES[:, :, 0:D]
        for h in range(H):
            V.tensor_tensor(RES[:, :, h * C:(h + 1) * C], RES[:, :, h * C:(h + 1) * C],
                            sm[:, :, h:h + 1].broadcast_to([BN, NB, C]), ALU.mult)
        dve.drain()
        V.tensor_tensor(y, y, SKIP[:], ALU.add)
        dve.drain()
        if last:
            V.tensor_tensor(X[:], X[:], y, ALU.add)
            dve.drain()
            layernorm(nc, dve, rooted, asked, X, mean, var, tmp, 1)

    finish_parts(g, name, work, (), n_sqrt=1 if last else 0)


def gcn_finish(g, name, bias, out):
    nc, X, RES, SKIP, cnt1 = (g[k] for k in ("nc", "X", "RES", "SKIP", "cnt1"))

    def work(dve, V, row, mean, var, tmp, sm, asked, rooted):
        y = RES[:, :, 0:D]
        V.tensor_tensor(y, y, SKIP[:], ALU.add)
        dve.drain()
        V.tensor_tensor(y, y, cnt1[:].unsqueeze(2).broadcast_to([BN, NB, D]), ALU.mult)
        dve.drain()
        V.tensor_tensor(y, y, rows_of(row[bias]), ALU.add)
        dve.drain()
        if out is None:
            V.tensor_scalar(y, y, 0.0, None, ALU.max)
        else:
            V.tensor_tensor(X[:], X[:], y, ALU.add)
            dve.drain()
            layernorm(nc, dve, rooted, asked, X, mean, var, tmp, 1)

    finish_parts(g, name, work, (bias,), n_sqrt=0 if out is None else 1, store=None if out is None else (X, out))


def kernel(**inputs):
    import numpy as np
    import concourse.bacc as bacc
    from concourse import mybir as mb
    from concourse.bass_utils import run_bass_kernel_spmd

    def padded(v, front, back, fill):
        v = np.asarray(v)
        out = np.full((front + v.shape[0] + back,) + v.shape[1:], fill, v.dtype)
        out[front:front + v.shape[0]] = v
        return out

    FAR = 1 << 20
    E_ROWS = 128 * (E // 128 + 1)
    arrays = {
        "x": padded(inputs["x"], 0, NP - N, 0),
        "src_p": padded(inputs["src"], 0, CH, 0),
        "dst_p": padded(inputs["dst"], 1, CH + 1, FAR),
        "dst_rows": padded(inputs["dst"], 0, E_ROWS - E, FAR).reshape(128, E_ROWS // 128),
        "src_cols": np.ascontiguousarray(padded(inputs["src"], 0, E_ROWS - E, 0).reshape(-1, 128).T),
        "dst_cols": np.ascontiguousarray(padded(inputs["dst"], 0, E_ROWS - E, FAR).reshape(-1, 128).T),
        "weight_cols": np.ascontiguousarray(padded(np.asarray(inputs["edge_weight1"]).reshape(E), 0, E_ROWS - E, 0).reshape(-1, 128).T),
        "attr_p": padded(inputs["edge_attr_13"], 0, CH, 0),
        "type_p": padded(inputs["edge_type_64"], 0, CH, 0),
        "weight_p": padded(np.asarray(inputs["edge_weight1"]).reshape(E), 0, CH, 0),
        "eye": np.eye(128, dtype=np.float32),
        "iota": np.arange(128, dtype=np.float32),
        "keys": np.arange(NP, dtype=np.float32),
        "more": np.arange(1, MORE + 1, dtype=np.float32) * np.float32(CH),
    }
    for k, v in inputs.items():
        if k[0] == "L":
            arrays[k] = np.ascontiguousarray(v)
    nc = bacc.Bacc("TRN2", target_bir_lowering=False, num_devices=1)
    arrays = {f"in_{k}": v for k, v in arrays.items()}
    aps = {k[3:]: nc.dram_tensor(k, v.shape, mb.dt.from_np(v.dtype), kind="ExternalInput").ap() for k, v in arrays.items()}
    out = nc.dram_tensor("out", (N, D), F32, kind="ExternalOutput").ap()
    build(nc, aps, out)
    r = run_bass_kernel_spmd(nc, [arrays], core_ids=[0])
    return r.results[0]["out"]
```
